# Optimizing a Trainium2 kernel written in Bass

```python
import numpy as np
import jax
import jax.numpy as jnp

def _softmax(x, axis=-1):
    return jax.nn.softmax(x, axis=axis)

def _gelu(x):
    return jax.nn.gelu(x, approximate=True)

def _silu(x):
    return jax.nn.silu(x)

def _sigmoid(x):
    return jax.nn.sigmoid(x)

def _layernorm(x, axis=-1, eps=1e-05):
    m = jnp.mean(x, axis=axis, keepdims=True)
    v = jnp.var(x, axis=axis, keepdims=True)
    return (x - m) / jnp.sqrt(v + eps)

def _scatter_add(tgt, idx, src, axis=0):
    return tgt.at[idx].add(src)

def _segment_sum(src, seg, n):
    return jax.ops.segment_sum(src, seg, n)
kernel_name = 'mk_xattn_ffn_d1_seqx_r8_81a49a'

def setup_inputs(seed: int=0):
    np.random.seed(seed)
    _w = jnp.asarray

    def _rec_inputs():
        import jax
        import jax.numpy as jnp
        _rk = jax.random.key(seed)
        x = 7.22e-05 + 1 * jax.random.normal(jax.random.fold_in(_rk, 1), (16, 128, 128), jnp.float32)
        _lenS = 128 - jax.random.randint(jax.random.fold_in(_rk, 7), (16,), 0, max(1, 128 // 4) + 1, jnp.int32)
        _lenS2 = 120 - jax.random.randint(jax.random.fold_in(_rk, 8), (16,), 0, max(1, 120 // 4) + 1, jnp.int32)
        _ctx_1024P = jax.random.normal(jax.random.fold_in(_rk, 11), (16, 16, 128), jnp.float32)
        _ctx_1024c = jax.random.dirichlet(jax.random.fold_in(_rk, 511), 0.3 * jnp.ones((16,), jnp.float32), (16, 120))
        _ctx_1024t = jnp.einsum('bsk,bkd->bsd', _ctx_1024c, _ctx_1024P)
        _ctx_1024t = _ctx_1024t * jax.lax.rsqrt(jnp.mean(jnp.square(_ctx_1024t)) + 1e-12) * 0.953939
        ctx_1024 = 4.13588e-05 + 0.999923 * (_ctx_1024t + 0.3 * jax.random.normal(jax.random.fold_in(_rk, 611), (16, 120, 128), jnp.float32))
        return (x, ctx_1024)
    x, ctx_1024 = _rec_inputs()

    def _L0_xattn_setup():
        import jax, jax.numpy as jnp
        import numpy as np
        DIM = 128
        key = jax.random.key(seed)
        ks = jax.random.split(key, 8)
        B, Sx, Sy, D = (4, 256, 256, DIM)
        s = 1.0 / np.sqrt(D)
        return {'x': jax.random.normal(ks[0], (B, Sx, D), jnp.float32), 'y': jax.random.normal(ks[1], (B, Sy, D), jnp.float32), 'Wq': jax.random.normal(ks[2], (D, D), jnp.float32) * s, 'bq': jnp.zeros((D,), jnp.float32), 'Wk': jax.random.normal(ks[3], (D, D), jnp.float32) * s, 'bk': jnp.zeros((D,), jnp.float32), 'Wv': jax.random.normal(ks[4], (D, D), jnp.float32) * s, 'bv': jnp.zeros((D,), jnp.float32)}
    _L0_xattn_all = _L0_xattn_setup()
    _L0_xattn_in = {k: v for k, v in _L0_xattn_all.items() if k in ('Wq', 'bq', 'Wk', 'bk', 'Wv', 'bv')}
    del _L0_xattn_all

    def _L0_ffn_setup():
        import jax, jax.numpy as jnp
        import numpy as np
        DIM = 128
        DEPTH = 6
        HEADS = 16
        DIM_HEAD = 64
        WINDOW = 32
        INNER = HEADS * DIM_HEAD
        DIM_INNER = int(DIM * 4 * 2 / 3)
        QK_SCALE = 8.0

        def shift_tokens(t):
            a, s = jnp.split(t, 2, -1)
            s = jnp.pad(s, ((0, 0), (1, 0), (0, 0)))[:, :-1]
            return jnp.concatenate([a, s], -1)

        def l2norm(t):
            return t / jnp.maximum(jnp.linalg.norm(t, axis=-1, keepdims=True), 1e-12)

        def rotate_half(x):
            x1, x2 = jnp.split(x, 2, -1)
            return jnp.concatenate([-x2, x1], -1)

        def rotary_tables(n):
            half = jnp.arange(0, DIM_HEAD, 2, dtype=jnp.float32)
            inv_freq = 1.0 / 10000.0 ** (half / DIM_HEAD)
            t = jnp.arange(n, dtype=jnp.float32)
            freqs = t[:, None] * inv_freq[None, :]
            freqs = jnp.concatenate([freqs, freqs], -1)
            base_scale = (half + 0.4 * DIM_HEAD) / (1.4 * DIM_HEAD)
            power = (t - n // 2) / (WINDOW // 2)
            scale = base_scale[None, :] ** power[:, None]
            scale = jnp.concatenate([scale, scale], -1)
            return (freqs, scale)

        def local_attention(q, k, v):
            b, h, n, d = q.shape
            w = WINDOW
            nw = n // w
            bq = q.reshape(b, h, nw, w, d)
            bk = k.reshape(b, h, nw, w, d)
            bv = v.reshape(b, h, nw, w, d)

            def look(t):
                p = jnp.pad(t, ((0, 0), (0, 0), (1, 0), (0, 0), (0, 0)))
                return jnp.concatenate([p[:, :, :nw], p[:, :, 1:]], axis=3)
            bk2, bv2 = (look(bk), look(bv))
            seq = jnp.arange(n).reshape(nw, w)
            seq_p = jnp.pad(seq, ((1, 0), (0, 0)), constant_values=-1)
            jt = jnp.concatenate([seq_p[:nw], seq_p[1:]], axis=1)
            it = seq[:, :, None]
            jb = jt[:, None, :]
            mask = (it < jb) | (it > jb + w) | (jb == -1)
            sim = jnp.einsum('bhwie,bhwje->bhwij', bq, bk2) * QK_SCALE
            sim = jnp.where(mask, -jnp.finfo(sim.dtype).max, sim)
            attn = jax.nn.softmax(sim, -1)
            out = jnp.einsum('bhwij,bhwje->bhwie', attn, bv2)
            return out.reshape(b, h, n, d)

        def attn_layer(x, Wqkv, qs, ksc, Wo):
            b, n, _ = x.shape
            qkv = x @ Wqkv
            q, k, v = jnp.split(qkv, 3, -1)
            sh = lambda t: t.reshape(b, n, HEADS, DIM_HEAD).transpose(0, 2, 1, 3)
            q, k, v = (sh(q), sh(k), sh(v))
            q = l2norm(q) * qs
            k = l2norm(k) * ksc
            freqs, scale = rotary_tables(n)
            cos, sin = (jnp.cos(freqs), jnp.sin(freqs))
            q = q * cos * scale + rotate_half(q) * sin * scale
            inv = 1.0 / scale
            k = k * cos * inv + rotate_half(k) * sin * inv
            out = local_attention(q, k, v)
            out = out.transpose(0, 2, 1, 3).reshape(b, n, INNER)
            return out @ Wo

        def ffn_layer(x, g, bln, W1, b1, W2, b2):
            mu = x.mean(-1, keepdims=True)
            var = ((x - mu) ** 2).mean(-1, keepdims=True)
            xn = (x - mu) / jnp.sqrt(var + 1e-05) * g + bln
            hg = xn @ W1 + b1
            a, gate = jnp.split(hg, 2, -1)
            return a * jax.nn.gelu(gate, approximate=False) @ W2 + b2
        key = jax.random.key(seed)
        ks = jax.random.split(key, 8)
        B, N = (2, 256)
        init = lambda k, shape: jax.random.normal(k, shape, jnp.float32) * 0.02
        return {'x': jax.random.normal(ks[0], (B, N, DIM), jnp.float32), 'Wqkv': init(ks[1], (DEPTH, DIM, 3 * INNER)), 'q_scale': jnp.ones((DEPTH, DIM_HEAD), jnp.float32), 'k_scale': jnp.ones((DEPTH, DIM_HEAD), jnp.float32), 'Wo': init(ks[2], (DEPTH, INNER, DIM)), 'ln_g': jnp.ones((DEPTH, DIM), jnp.float32), 'ln_b': jnp.zeros((DEPTH, DIM), jnp.float32), 'W1': init(ks[3], (DEPTH, DIM, 2 * DIM_INNER)), 'b1': jnp.zeros((DEPTH, 2 * DIM_INNER), jnp.float32), 'W2': init(ks[4], (DEPTH, DIM_INNER, DIM)), 'b2': jnp.zeros((DEPTH, DIM), jnp.float32)}
    _L0_ffn_all = _L0_ffn_setup()
    _L0_ffn_in = {k: v for k, v in _L0_ffn_all.items() if k in ('Wqkv', 'q_scale', 'k_scale', 'Wo', 'ln_g', 'ln_b', 'W1', 'b1', 'W2', 'b2')}
    del _L0_ffn_all
    return {'x': x, 'ctx_1024': ctx_1024, 'L0_xattn_Wq': _L0_xattn_in['Wq'], 'L0_xattn_bq': _L0_xattn_in['bq'], 'L0_xattn_Wk': _L0_xattn_in['Wk'], 'L0_xattn_bk': _L0_xattn_in['bk'], 'L0_xattn_Wv': _L0_xattn_in['Wv'], 'L0_xattn_bv': _L0_xattn_in['bv'], 'L0_ffn_Wqkv': _L0_ffn_in['Wqkv'], 'L0_ffn_q_scale': _L0_ffn_in['q_scale'], 'L0_ffn_k_scale': _L0_ffn_in['k_scale'], 'L0_ffn_Wo': _L0_ffn_in['Wo'], 'L0_ffn_ln_g': _L0_ffn_in['ln_g'], 'L0_ffn_ln_b': _L0_ffn_in['ln_b'], 'L0_ffn_W1': _L0_ffn_in['W1'], 'L0_ffn_b1': _L0_ffn_in['b1'], 'L0_ffn_W2': _L0_ffn_in['W2'], 'L0_ffn_b2': _L0_ffn_in['b2']}

def reference(x, ctx_1024, L0_xattn_Wq, L0_xattn_bq, L0_xattn_Wk, L0_xattn_bk, L0_xattn_Wv, L0_xattn_bv, L0_ffn_Wqkv, L0_ffn_q_scale, L0_ffn_k_scale, L0_ffn_Wo, L0_ffn_ln_g, L0_ffn_ln_b, L0_ffn_W1, L0_ffn_b1, L0_ffn_W2, L0_ffn_b2):
    import jax
    import jax.numpy as jnp

    def _L0_xattn_ref(x, y, Wq, bq, Wk, bk, Wv, bv):
        import jax, jax.numpy as jnp
        import numpy as np
        DIM = 128
        D = x.shape[-1]
        scale = jnp.sqrt(jnp.asarray(D, x.dtype))
        Q = jnp.einsum('bsd,de->bse', x, Wq) + bq
        K = jnp.einsum('btd,de->bte', y, Wk) + bk
        V = jnp.einsum('btd,de->bte', y, Wv) + bv
        scores = jnp.einsum('bse,bte->bst', Q, K) / scale
        probs = jax.nn.softmax(scores, axis=-1)
        out = jnp.einsum('bst,bte->bse', probs, V)
        return out

    def _L0_ffn_ref(x, Wqkv, q_scale, k_scale, Wo, ln_g, ln_b, W1, b1, W2, b2):
        import jax, jax.numpy as jnp
        import numpy as np
        DIM = 128
        DEPTH = 6
        HEADS = 16
        DIM_HEAD = 64
        WINDOW = 32
        INNER = HEADS * DIM_HEAD
        DIM_INNER = int(DIM * 4 * 2 / 3)
        QK_SCALE = 8.0

        def shift_tokens(t):
            a, s = jnp.split(t, 2, -1)
            s = jnp.pad(s, ((0, 0), (1, 0), (0, 0)))[:, :-1]
            return jnp.concatenate([a, s], -1)

        def l2norm(t):
            return t / jnp.maximum(jnp.linalg.norm(t, axis=-1, keepdims=True), 1e-12)

        def rotate_half(x):
            x1, x2 = jnp.split(x, 2, -1)
            return jnp.concatenate([-x2, x1], -1)

        def rotary_tables(n):
            half = jnp.arange(0, DIM_HEAD, 2, dtype=jnp.float32)
            inv_freq = 1.0 / 10000.0 ** (half / DIM_HEAD)
            t = jnp.arange(n, dtype=jnp.float32)
            freqs = t[:, None] * inv_freq[None, :]
            freqs = jnp.concatenate([freqs, freqs], -1)
            base_scale = (half + 0.4 * DIM_HEAD) / (1.4 * DIM_HEAD)
            power = (t - n // 2) / (WINDOW // 2)
            scale = base_scale[None, :] ** power[:, None]
            scale = jnp.concatenate([scale, scale], -1)
            return (freqs, scale)

        def local_attention(q, k, v):
            b, h, n, d = q.shape
            w = WINDOW
            nw = n // w
            bq = q.reshape(b, h, nw, w, d)
            bk = k.reshape(b, h, nw, w, d)
            bv = v.reshape(b, h, nw, w, d)

            def look(t):
                p = jnp.pad(t, ((0, 0), (0, 0), (1, 0), (0, 0), (0, 0)))
                return jnp.concatenate([p[:, :, :nw], p[:, :, 1:]], axis=3)
            bk2, bv2 = (look(bk), look(bv))
            seq = jnp.arange(n).reshape(nw, w)
            seq_p = jnp.pad(seq, ((1, 0), (0, 0)), constant_values=-1)
            jt = jnp.concatenate([seq_p[:nw], seq_p[1:]], axis=1)
            it = seq[:, :, None]
            jb = jt[:, None, :]
            mask = (it < jb) | (it > jb + w) | (jb == -1)
            sim = jnp.einsum('bhwie,bhwje->bhwij', bq, bk2) * QK_SCALE
            sim = jnp.where(mask, -jnp.finfo(sim.dtype).max, sim)
            attn = jax.nn.softmax(sim, -1)
            out = jnp.einsum('bhwij,bhwje->bhwie', attn, bv2)
            return out.reshape(b, h, n, d)

        def attn_layer(x, Wqkv, qs, ksc, Wo):
            b, n, _ = x.shape
            qkv = x @ Wqkv
            q, k, v = jnp.split(qkv, 3, -1)
            sh = lambda t: t.reshape(b, n, HEADS, DIM_HEAD).transpose(0, 2, 1, 3)
            q, k, v = (sh(q), sh(k), sh(v))
            q = l2norm(q) * qs
            k = l2norm(k) * ksc
            freqs, scale = rotary_tables(n)
            cos, sin = (jnp.cos(freqs), jnp.sin(freqs))
            q = q * cos * scale + rotate_half(q) * sin * scale
            inv = 1.0 / scale
            k = k * cos * inv + rotate_half(k) * sin * inv
            out = local_attention(q, k, v)
            out = out.transpose(0, 2, 1, 3).reshape(b, n, INNER)
            return out @ Wo

        def ffn_layer(x, g, bln, W1, b1, W2, b2):
            mu = x.mean(-1, keepdims=True)
            var = ((x - mu) ** 2).mean(-1, keepdims=True)
            xn = (x - mu) / jnp.sqrt(var + 1e-05) * g + bln
            hg = xn @ W1 + b1
            a, gate = jnp.split(hg, 2, -1)
            return a * jax.nn.gelu(gate, approximate=False) @ W2 + b2
        for i in range(DEPTH):
            x = attn_layer(shift_tokens(x), Wqkv[i], q_scale[i], k_scale[i], Wo[i]) + x
            x = ffn_layer(shift_tokens(x), ln_g[i], ln_b[i], W1[i], b1[i], W2[i], b2[i]) + x
        return x
    x = x + _L0_xattn_ref(_layernorm(x, axis=-1), ctx_1024, L0_xattn_Wq, L0_xattn_bq, L0_xattn_Wk, L0_xattn_bk, L0_xattn_Wv, L0_xattn_bv)
    x = x + _L0_ffn_ref(_layernorm(x, axis=-1), L0_ffn_Wqkv, L0_ffn_q_scale, L0_ffn_k_scale, L0_ffn_Wo, L0_ffn_ln_g, L0_ffn_ln_b, L0_ffn_W1, L0_ffn_b1, L0_ffn_W2, L0_ffn_b2)
    return x

_drawn_inputs = setup_inputs


def setup_inputs(seed=0):
    import zlib

    import numpy as np

    out = dict(_drawn_inputs(seed))
    spreads = {'L0_xattn_bq': (0.0, 0.356),
     'L0_xattn_bk': (0.0, 0.8),
     'L0_xattn_bv': (0.0, 0.1),
     'L0_ffn_q_scale': (1.0, 0.6),
     'L0_ffn_k_scale': (1.0, 0.6),
     'L0_ffn_ln_g': (1.0, 0.6),
     'L0_ffn_ln_b': (0.0, 0.8),
     'L0_ffn_b1': (0.0, 0.8),
     'L0_ffn_b2': (0.0, 0.1)}
    factors = {'L0_ffn_W1': 3.967, 'L0_ffn_W2': 3.89}
    for name, (base, spread) in spreads.items():
        noise = np.random.default_rng([zlib.crc32(name.encode()), seed]).standard_normal(out[name].shape)
        drawn = base * np.exp(spread * noise) if base else spread * noise
        out[name] = jnp.asarray(drawn.astype(out[name].dtype))
    for name, factor in factors.items():
        out[name] = (out[name] * factor).astype(out[name].dtype)
    return out
```

```python
import numpy as np
import concourse.bass as bass
from concourse import mybir
from concourse.alu_op_type import AluOpType as ALU

F32 = mybir.dt.float32
BF16 = mybir.dt.bfloat16
ACT = mybir.ActivationFunctionType
AX = mybir.AxisListType

P = 128
B = 16
CT = 120
L = 6
H = 16
E = 64
WIN = 32
INNER = H * E
FI = 341
FCH = 3
FC = 114
QUAD = 4
NQ = B // QUAD
EPS = 1e-5
QK_SCALE = 8.0
MASKED = -1e30
LN_SHIFT = 2.0 ** 20

CHUNK_COLS = [0, INNER, 512, INNER + 512, 2 * INNER, 2 * INNER + 512]
Q0, K0, Q1, K1, V0, V1 = range(6)


def head(g, k):
    return 8 * (g // 2) + 2 * k + g % 2


def constants():
    half = np.arange(0, E, 2, dtype=np.float32)
    inv_freq = (np.float32(1.0) / np.power(np.float32(10000.0), half / np.float32(E))).astype(np.float32)
    t = np.arange(P, dtype=np.float32)
    fr = (t[:, None] * inv_freq[None, :]).astype(np.float32)
    fr = np.concatenate([fr, fr], -1)
    base = ((half + np.float32(0.4 * E)) / np.float32(1.4 * E)).astype(np.float32)
    power = ((t - P // 2) / np.float32(WIN // 2)).astype(np.float32)
    sc = np.power(base[None, :], power[:, None]).astype(np.float32)
    sc = np.concatenate([sc, sc], -1)
    cos, sin = np.cos(fr).astype(np.float32), np.sin(fr).astype(np.float32)
    sign = np.where(np.arange(E) < E // 2, -1.0, 1.0).astype(np.float32)
    inv = (np.float32(1.0) / sc).astype(np.float32)
    rope = np.stack([cos * sc * QK_SCALE, sin * sc * sign * QK_SCALE, cos * inv, sin * inv * sign], 1)
    q, k = np.arange(P)[:, None], np.arange(P)[None, :]
    band = np.where((k <= q) & (q <= k + WIN), 0.0, MASKED).astype(np.float32)
    ident = np.eye(P, dtype=np.float32)
    shift = np.eye(P, k=1, dtype=np.float32)
    return rope.astype(np.float32), np.concatenate([band, ident, shift], 1)


def build(nc, x_d, ctx_d, xw_d, xv_d, bv_d, wqkv_d, qk_scale_d, wo_d, w1_d, w2_d, vec_d, b2_d, rope_d, const_d, out_d):
    def sb(name, shape, dt=F32):
        return nc.alloc_sbuf_tensor(name, shape, dt)

    x1 = sb("x1", [P, B, P])
    xr = sb("xr", [P, B, P])
    wqkv = sb("wqkv", [P, 3 * INNER])
    wo = sb("wo", [P, 8, P])
    w1 = sb("w1", [P, 2 * FCH, FC])
    w2 = sb("w2", [FC, FCH, P])
    vec = sb("vec", [P, 2 + 2 * FCH])
    b2 = sb("b2", [1, P])
    qks = sb("qks", [P, 2, E])
    rope_base = sb("rope_base", [P, 4, E])
    rope = sb("rope", [P, 4, E])
    consts = sb("consts", [P, 3 * P])
    ident = consts[:, P:2 * P]
    shift = consts[:, 2 * P:3 * P]
    ident16 = sb("ident16", [P, P], BF16)
    band16 = sb("band16", [P, 4, P], BF16)
    ones = sb("ones", [1, P])
    half_shift = sb("half_shift", [P, 1])
    three_halves = sb("three_halves", [P, 16])
    minus_half = sb("minus_half", [P, QUAD])
    xs = sb("xs", [P, 2, P])
    xt = sb("xt", [P, 2, P])
    sq = sb("sq", [P, 2, 512])
    ss = sb("ss", [P, 2, 2, 8])
    rn = sb("rn", [P, 2, 2, 8])
    nt = sb("nt", [P, 2, 16])
    t1 = sb("t1", [P, 4, 512])
    t2 = sb("t2", [P, 4, 512])
    qT = sb("qT", [P, 2, 8, P])
    kT = sb("kT", [P, 2, 8, P])
    v = sb("v", [P, 2, INNER])
    nmax = sb("nmax", [P, 4, 4])
    psums = sb("psums", [P, 4, 4])
    rsum = sb("rsum", [P, 4, 4])
    pr = sb("pr", [P, 2, 4, P])
    pT = sb("pT", [P, 4, 4, P])
    oT = sb("oT", [P, 8, P])
    st = sb("st", [P, 2, QUAD, 6])
    mv = sb("mv", [P, 2, QUAD, 2])
    rstd = sb("rstd", [P, 2, QUAD])
    xh = sb("xh", [P, QUAD, P])
    xhT = sb("xhT", [P, 2, QUAD * P])
    gate = sb("gate", [FC, 2, QUAD * P])
    hT = sb("hT", [FC, 2, FCH, QUAD * P])
    xw = sb("xw", [P, 3, P])
    xvec = sb("xvec", [P, 2])
    bv = sb("bv", [1, P])
    ctx = sb("ctx", [CT, 2, QUAD, P])
    ctxT = sb("ctxT", [P, QUAD * CT])
    xq = sb("xq", [P, QUAD * P])
    xk = sb("xk", [P, QUAD * CT])
    xvv = sb("xvv", [CT, QUAD, P])

    ps = nc.alloc_psum_tensor("ps", [P, 8, 512], F32)
    QKV_BANK = [0, 1, 2]
    S_BANK = [3, 4]
    T_BANK = [5, 6]
    O_BANK = 7

    def sem(name):
        return nc.alloc_semaphore(name)

    ld_const, ld_qkv, ld_wo, ld_ffn = (sem(s) for s in ("ld_const", "ld_qkv", "ld_wo", "ld_ffn"))
    ld_x = [sem(f"ld_x{q}") for q in range(NQ)]
    ld_ctx = [sem(f"ld_ctx{q}") for q in range(2)]
    const_ready, x_final = sem("const_ready"), sem("x_final")
    rope_ready = sem("rope_ready")
    xs_ready, xt_ps, xt_ready = sem("xs_ready"), sem("xt_ps"), sem("xt_ready")
    qkv_ps, sq_ready, ss_ready, ss_clamped, rope_done, rn_guess, v_ready = (
        sem(s) for s in ("qkv_ps", "sq_ready", "ss_ready", "ss_clamped", "rope_done", "rn_guess", "v_ready"))
    newton, qk_added, qk_ready, tq_ps, tq_ready = (sem(s) for s in ("newton", "qk_added", "qk_ready", "tq_ps", "tq_ready"))
    s_ps, max_ready, exp_ready, rsum_ready, pr_ready, pt_ps, pt_ready, o_ps, o_ready, y_ps, x_updated = (
        sem(s) for s in ("s_ps", "max_ready", "exp_ready", "rsum_ready", "pr_ready", "pt_ps", "pt_ready", "o_ps", "o_ready", "y_ps", "x_updated"))
    ln_self = sem("ln_self")
    f_shift_ps, f_stats, f_var, f_pow, f_rstd, f_xh, f_xhT_ps, f_xhT, f_h_ps, f_gate, f_h, f_y_ps = (
        sem("f_" + s) for s in ("shift_ps", "stats", "var", "pow", "rstd", "xh", "xhT_ps", "xhT", "h_ps", "gate", "h", "y_ps"))
    c_stats, c_var, c_rstd, c_xn, c_tr_ps, c_tr, c_qk_ps, c_qk, c_s_ps, c_max, c_exp, c_sum, c_pn, c_pT_ps, c_pT, c_o_ps, c_x1 = (
        sem("c_" + s) for s in ("stats", "var", "rstd", "xn", "tr_ps", "tr", "qk_ps", "qk", "s_ps", "max", "exp", "sum", "pn", "pT_ps", "pT", "o_ps", "x1"))
    final_sum, stored, passed = sem("final_sum"), sem("stored"), sem("passed")

    PAIRS = B // 2

    def count(l, b, per, k):
        return l * (B * per) + b * per + k

    def wait_apart(eng, semaphore, value):
        eng.wait_ge(semaphore, value)
        eng.sem_inc(passed, 1)

    block = nc.Block()
    with block as block:

        @block.sync
        def _(sp):
            sp.dma_start(x1[:, 0:QUAD, :], x_d[0:QUAD].rearrange("b t d -> t b d")).then_inc(ld_x[0], 16)
            sp.dma_start(consts[:], const_d).then_inc(ld_const, 16)
            sp.dma_start(xw[:], xw_d).then_inc(ld_const, 16)
            sp.dma_start(xvec[:], xv_d).then_inc(ld_const, 16)
            sp.dma_start(bv[:], bv_d).then_inc(ld_const, 16)
            sp.dma_start(rope_base[:], rope_d).then_inc(ld_const, 16)
            for q in range(NQ):
                if q >= 2:
                    sp.wait_ge(c_tr_ps, 2 * (q - 2) + 2)
                sp.dma_start(ctx[:, q % 2], ctx_d[q * QUAD:(q + 1) * QUAD].rearrange("b t d -> t b d")).then_inc(ld_ctx[q % 2], 16)
                if q + 1 < NQ:
                    s = slice((q + 1) * QUAD, (q + 2) * QUAD)
                    sp.dma_start(x1[:, s, :], x_d[s].rearrange("b t d -> t b d")).then_inc(ld_x[q + 1], 16)

            def load_attention(l):
                sp.dma_start(wqkv[:], wqkv_d[l]).then_inc(ld_qkv, 16)
                sp.dma_start(qks[:], qk_scale_d[l].unsqueeze(0).broadcast_to([P, 2, E])).then_inc(ld_qkv, 16)

            def load_rest(l):
                sp.dma_start(w1[:], w1_d[l]).then_inc(ld_ffn, 16)
                sp.dma_start(w2[:], w2_d[l]).then_inc(ld_ffn, 16)
                sp.dma_start(vec[:], vec_d[l]).then_inc(ld_ffn, 16)
                sp.dma_start(b2[:], b2_d[l]).then_inc(ld_ffn, 16)

            load_attention(0)
            sp.dma_start(wo[:], wo_d[0]).then_inc(ld_wo, 16)
            load_rest(0)
            with sp.Fori(1, L) as l:
                wait_apart(sp, qkv_ps, count(l, 0, 6, 0))
                wait_apart(sp, rope_ready, l * 4)
                load_attention(l)
                wait_apart(sp, y_ps, count(l, 0, 1, 0))
                sp.dma_start(wo[:], wo_d[l]).then_inc(ld_wo, 16)
                wait_apart(sp, f_y_ps, l * NQ)
                wait_apart(sp, f_h, l * NQ * FCH)
                load_rest(l)
            for q in range(NQ):
                sp.wait_ge(final_sum, q + 1)
                s = slice(q * QUAD, (q + 1) * QUAD)
                sp.dma_start(out_d[s].rearrange("b t d -> t b d"), x1[:, s, :]).then_inc(stored, 16)
            sp.wait_ge(stored, 16 * NQ)

        @block.tensor
        def _(pe):
            mm, tr = nc.tensor.matmul, nc.tensor.transpose

            def cross_attention(q):
                pe.wait_ge(c_xn, q + 1)
                if q >= 1:
                    pe.wait_ge(c_x1, q)
                for b in range(QUAD):
                    i = tr(ps[:, 0, b * P:(b + 1) * P], xh[:, b, :], ident)
                i.then_inc(c_tr_ps, 1)
                pe.wait_ge(ld_ctx[q % 2], 16 * (q // 2 + 1))
                for b in range(QUAD):
                    i = tr(ps[:, 1, b * CT:(b + 1) * CT], ctx[:, q % 2, b, :], ident[0:CT, 0:CT])
                i.then_inc(c_tr_ps, 1)
                pe.wait_ge(c_tr, 2 * q + 1)
                mm(ps[:, 2, :], xw[:, 0, :], xhT[:, 0, :], start=True, stop=True).then_inc(c_qk_ps, 1)
                pe.wait_ge(c_tr, 2 * q + 2)
                mm(ps[:, 3, 0:QUAD * CT], xw[:, 1, :], ctxT[:], start=True, stop=True).then_inc(c_qk_ps, 1)
                for b in range(QUAD):
                    o = ps[0:CT, 4, b * P:(b + 1) * P]
                    mm(o, ctxT[:, b * CT:(b + 1) * CT], xw[:, 2, :], start=True, stop=False)
                    i = mm(o, ones[0:1, 0:CT], bv[:], start=False, stop=True)
                i.then_inc(c_qk_ps, 1)
                pe.wait_ge(c_qk, 3 * q + 2)
                for b in range(QUAD):
                    i = mm(ps[:, 5, b * P:b * P + CT], xq[:, b * P:(b + 1) * P], xk[:, b * CT:(b + 1) * CT], start=True, stop=True)
                i.then_inc(c_s_ps, 1)
                pe.wait_ge(c_pn, q + 1)
                for b in range(QUAD):
                    i = tr(ps[0:CT, 6, b * P:(b + 1) * P], pr[:, 0, b, 0:CT], ident)
                i.then_inc(c_pT_ps, 1)
                pe.wait_ge(c_pT, q + 1)
                pe.wait_ge(c_qk, 3 * q + 3)
                for b in range(QUAD):
                    i = mm(ps[:, 7, b * P:(b + 1) * P], pT[0:CT, 0, b, :], xvv[:, b, :], start=True, stop=True)
                i.then_inc(c_o_ps, 1)

            def transpose_x(l, b, par, first=False):
                if not first:
                    pe.wait_ge(x_updated, count(l, b, 1, -2 + 1))
                pe.wait_ge(xs_ready, count(l, b, 1, 1))
                tr(ps[:, O_BANK, 0:P], xs[:, par, :], ident).then_inc(xt_ps, 1)

            def project(l, b, par, c):
                if c == Q0:
                    pe.wait_ge(xt_ready, count(l, b, 2, 2))
                mm(ps[:, QKV_BANK[c % 3], :], xt[:, par, :], wqkv[:, CHUNK_COLS[c]:CHUNK_COLS[c] + 512],
                   start=True, stop=True).then_inc(qkv_ps, 1)

            def transpose_qk(l, b, c):
                pe.wait_ge(qk_ready, count(l, b, 4, c + 1))
                for k in range(4):
                    i = tr(ps[:, T_BANK[c % 2], k * P:(k + 1) * P], t1[:, c, k * P:(k + 1) * P], ident)
                i.then_inc(tq_ps, 1)

            def scores(l, b, par, g):
                pe.wait_ge(tq_ready, count(l, b, 4, 2 * (g // 2) + 2))
                if g >= 2:
                    pe.wait_ge(exp_ready, count(l, b, 4, g - 1))
                o = S_BANK[g % 2]
                mm(ps[:, o, :], ident16[:], band16[:].rearrange("p a k -> p (a k)"), start=True, stop=False, skip_group_check=True)
                for k in range(4):
                    h = head(g, k)
                    r = slice(E * (h % 2), E * (h % 2) + E)
                    i = mm(ps[:, o, k * P:(k + 1) * P], qT[r, par, h // 2, :], kT[r, par, h // 2, :], start=False, stop=k == 3,
                           skip_group_check=True)
                i.then_inc(s_ps, 1)

            def transpose_p(l, b, g):
                pe.wait_ge(pr_ready, count(l, b, 4, g + 1))
                if g < 2:
                    pe.wait_ge(tq_ready, count(l, b, 4, g + 3))
                else:
                    pe.wait_ge(pt_ready, count(l, b, 4, g - 1))
                for k in range(4):
                    i = tr(ps[:, T_BANK[g % 2], k * P:(k + 1) * P], pr[:, g % 2, k, :], ident)
                i.then_inc(pt_ps, 1)

            def weigh_values(l, b, par, s, after_x):
                pe.wait_ge(pt_ready, count(l, b, 4, 2 * s + 2))
                if s == 0:
                    pe.wait_ge(v_ready, count(l, b, 2, 2))
                    pe.wait_ge(x_updated, count(l, b, 1, 1))
                    if after_x:
                        pe.wait_ge(xt_ready, count(l, b + 2, 2, 2))
                else:
                    pe.wait_ge(o_ready, count(l, b, 2, 1))
                for k in range(4):
                    for odd in range(2):
                        g = 2 * s + odd
                        h = head(g, k)
                        i = mm(ps[odd * E:odd * E + E, O_BANK, k * P:(k + 1) * P], v[:, par, h * E:(h + 1) * E], pT[:, g, k, :],
                               start=True, stop=True)
                i.then_inc(o_ps, 1)

            def output_projection(l, b):
                pe.wait_ge(o_ready, count(l, b, 2, 2))
                for c in range(8):
                    i = mm(ps[:, O_BANK, 0:P], oT[:, c, :], wo[:, c, :], start=c == 0, stop=c == 7)
                i.then_inc(y_ps, 1)

            def attention(l, b, par, nxt=True, nxt2=True):
                n = b + 1
                scores(l, b, par, 0)
                scores(l, b, par, 1)
                if nxt2:
                    transpose_x(l, b + 2, par)
                if nxt:
                    pe.wait_ge(rope_done, count(l, b, 4, 4))
                    project(l, n, 1 - par, Q0)
                    pe.wait_ge(v_ready, count(l, b, 2, 2))
                    project(l, n, 1 - par, K0)
                pe.wait_ge(tq_ready, count(l, b, 4, 2))
                transpose_qk(l, b, Q1)
                transpose_qk(l, b, K1)
                transpose_p(l, b, 0)
                if nxt:
                    project(l, n, 1 - par, Q1)
                scores(l, b, par, 2)
                transpose_p(l, b, 1)
                if nxt:
                    pe.wait_ge(rope_done, count(l, n, 4, 1))
                    project(l, n, 1 - par, K1)
                weigh_values(l, b, par, 0, nxt2)
                scores(l, b, par, 3)
                if nxt:
                    pe.wait_ge(rope_done, count(l, n, 4, 2))
                    project(l, n, 1 - par, V0)
                transpose_p(l, b, 2)
                if nxt:
                    pe.wait_ge(rope_done, count(l, n, 4, 3))
                    project(l, n, 1 - par, V1)
                transpose_p(l, b, 3)
                if nxt:
                    pe.wait_ge(pt_ready, count(l, b, 4, 4))
                    transpose_qk(l, n, Q0)
                    transpose_qk(l, n, K0)
                weigh_values(l, b, par, 1, nxt2)
                output_projection(l, b)

            def ffn_shift(l, q):
                pe.wait_ge(x_updated, count(l, QUAD * q + QUAD - 1, 1, 2))
                if q >= 2:
                    pe.wait_ge(f_xh, l * NQ + q - 1)
                s = slice(q * QUAD, (q + 1) * QUAD)
                o = ps[:, q % 2, :].rearrange("p (b d) -> p b d", b=QUAD)
                mm(o[:, :, 0:E], ident, xr[:, s, 0:E], start=True, stop=True)
                mm(o[:, :, E:P], shift, xr[:, s, E:P], start=True, stop=True).then_inc(f_shift_ps, 1)

            def ffn_transpose(l, q):
                pe.wait_ge(f_xh, l * NQ + q + 1)
                if q >= 1:
                    pe.wait_ge(f_xhT, l * NQ + q)
                for b in range(QUAD):
                    i = tr(ps[:, 5, b * P:(b + 1) * P], xh[:, b, :], ident)
                i.then_inc(f_xhT_ps, 1)

            def ffn_up(l, q, c):
                j = q * FCH + c
                if c == 0:
                    pe.wait_ge(f_xhT, l * NQ + q + 1)
                if j >= 2:
                    pe.wait_ge(f_h, (l * NQ + q) * FCH + c - 1)
                mm(ps[0:FC, [4, 7][j % 2], :], w1[:, FCH + c, :], xhT[:, q % 2, :], start=True, stop=True)
                mm(ps[0:FC, 2 + j % 2, :], w1[:, c, :], xhT[:, q % 2, :], start=True, stop=True).then_inc(f_h_ps, 1)

            def ffn_down(l, q):
                pe.wait_ge(f_h, (l * NQ + q + 1) * FCH)
                if q >= 1:
                    pe.wait_ge(x_final, (l + 1) * NQ + q)
                for b in range(QUAD):
                    o = ps[:, 6, b * P:(b + 1) * P]
                    for c in range(FCH):
                        mm(o, hT[:, q % 2, c, b * P:(b + 1) * P], w2[:, c, :], start=c == 0, stop=False)
                    i = mm(o, ones[:], b2[:], start=False, stop=True)
                i.then_inc(f_y_ps, 1)

            pe.wait_ge(ld_const, 80)
            pe.wait_ge(const_ready, 7)
            for q in range(NQ):
                cross_attention(q)
            with pe.Fori(0, L) as l:
                pe.wait_ge(x_final, (l + 1) * NQ)
                transpose_x(l, 0, 0, first=True)
                pe.wait_ge(xt_ready, count(l, 0, 2, 2))
                transpose_x(l, 1, 1, first=True)
                pe.wait_ge(ld_qkv, 32 * l + 32)
                project(l, 0, 0, Q0)
                project(l, 0, 0, K0)
                project(l, 0, 0, Q1)
                pe.wait_ge(rope_done, count(l, 0, 4, 1))
                project(l, 0, 0, K1)
                pe.wait_ge(rope_done, count(l, 0, 4, 2))
                project(l, 0, 0, V0)
                pe.wait_ge(rope_done, count(l, 0, 4, 3))
                project(l, 0, 0, V1)
                transpose_qk(l, 0, Q0)
                transpose_qk(l, 0, K0)
                wait_apart(pe, ld_wo, 16 * l + 16)
                with pe.Fori(0, PAIRS - 1) as j:
                    attention(l, 2 * j, 0)
                    attention(l, 2 * j + 1, 1)
                attention(l, B - 2, 0, nxt2=False)
                attention(l, B - 1, 1, nxt=False, nxt2=False)

                ffn_shift(l, 0)
                ffn_shift(l, 1)
                ffn_transpose(l, 0)
                pe.wait_ge(ld_ffn, 64 * l + 64)
                for q in range(NQ + 1):
                    if q < NQ:
                        ffn_up(l, q, 0)
                    if q >= 1:
                        ffn_down(l, q - 1)
                    if q < NQ:
                        ffn_up(l, q, 1)
                        ffn_up(l, q, 2)
                    if q + 1 < NQ:
                        ffn_transpose(l, q + 1)
                    if q + 2 < NQ:
                        ffn_shift(l, q + 2)

        @block.scalar
        def _(act):
            A = nc.scalar.activation

            def cross_attention(q):
                act.wait_ge(c_tr_ps, 2 * q + 1)
                A(xhT[:, 0, :], ps[:, 0, :], ACT.Copy).then_inc(c_tr, 1)
                act.wait_ge(c_tr_ps, 2 * q + 2)
                A(ctxT[:], ps[:, 1, 0:QUAD * CT], ACT.Copy).then_inc(c_tr, 1)
                act.wait_ge(c_qk_ps, 3 * q + 1)
                A(xq[:], ps[:, 2, :], ACT.Identity, bias=xvec[:, 0:1]).then_inc(c_qk, 1)
                act.wait_ge(c_qk_ps, 3 * q + 2)
                A(xk[:], ps[:, 3, 0:QUAD * CT], ACT.Identity, bias=xvec[:, 1:2]).then_inc(c_qk, 1)
                act.wait_ge(c_qk_ps, 3 * q + 3)
                A(xvv[:].rearrange("p b d -> p (b d)"), ps[0:CT, 4, :], ACT.Copy).then_inc(c_qk, 1)
                act.wait_ge(c_max, 2 * q + 2)
                for b in range(QUAD):
                    A(pr[:, 0, b, 0:CT], ps[:, 5, b * P:b * P + CT], ACT.Exp, bias=nmax[:, 1, b:b + 1],
                      scale=float(P) ** -0.5, accum_out=psums[:, 0, b:b + 1]).then_inc(c_exp, 1)
                act.wait_ge(c_pT_ps, q + 1)
                A(pT[0:CT, 0].rearrange("p b d -> p (b d)"), ps[0:CT, 6, :], ACT.Copy).then_inc(c_pT, 1)

            def copy_xt(l, b, par):
                act.wait_ge(xt_ps, count(l, b, 1, 1))
                A(xt[0:E, par, :], ps[0:E, O_BANK, 0:P], ACT.Copy).then_inc(xt_ready, 1)
                A(xt[E:P, par, 1:P], ps[E:P, O_BANK, 0:P - 1], ACT.Copy).then_inc(xt_ready, 1)

            def square(l, b, c):
                act.wait_ge(qkv_ps, count(l, b, 6, c + 1))
                if c >= 2:
                    act.wait_ge(ss_ready, count(l, b, 4, c - 1))
                A(sq[:, c % 2, :], ps[:, QKV_BANK[c % 3], :], ACT.Square).then_inc(sq_ready, 1)

            def guess_norm(l, b, u):
                act.wait_ge(ss_clamped, count(l, b, 2, u + 1))
                r = rn[:, u].rearrange("p a h -> p (a h)")
                A(r, ss[:, u].rearrange("p a h -> p (a h)"), ACT.Ln, scale=-2.0 * LN_SHIFT).then_inc(ln_self, 1)
                act.wait_ge(ln_self, count(l, b, 2, u + 1))
                A(r, r, ACT.Exp, scale=-0.5, bias=half_shift[:, 0:1]).then_inc(rn_guess, 1)

            def copy_v(l, b, par, c):
                act.wait_ge(qkv_ps, count(l, b, 6, c + 1))
                A(v[:, par, (c - V0) * 512:(c - V0 + 1) * 512], ps[:, QKV_BANK[c % 3], :], ACT.Copy).then_inc(v_ready, 1)

            def copy_qk(l, b, par, c):
                act.wait_ge(tq_ps, count(l, b, 4, c + 1))
                dst = (qT, kT)[c % 2]
                A(dst[:, par, 4 * (c // 2):4 * (c // 2) + 4, :].rearrange("p a t -> p (a t)"), ps[:, T_BANK[c % 2], :],
                  ACT.Copy).then_inc(tq_ready, 1)

            def exps(l, b, g):
                act.wait_ge(max_ready, count(l, b, 4, g + 1))
                if g >= 2:
                    act.wait_ge(pt_ps, count(l, b, 4, g - 1))
                for k in range(4):
                    i = A(pr[:, g % 2, k, :], ps[:, S_BANK[g % 2], k * P:(k + 1) * P], ACT.Exp, bias=nmax[:, g, k:k + 1],
                          accum_out=psums[:, g, k:k + 1])
                i.then_inc(exp_ready, 1)

            def copy_o(l, b, s):
                act.wait_ge(o_ps, count(l, b, 2, s + 1))
                A(oT[:, 4 * s:4 * s + 4, :].rearrange("p a t -> p (a t)"), ps[:, O_BANK, :], ACT.Copy).then_inc(o_ready, 1)

            def attention(l, b, par, nxt=True, nxt2=True):
                n = b + 1
                exps(l, b, 0)
                if nxt2:
                    copy_xt(l, b + 2, par)
                if nxt:
                    square(l, n, Q0)
                exps(l, b, 1)
                if nxt:
                    square(l, n, K0)
                copy_qk(l, b, par, Q1)
                copy_qk(l, b, par, K1)
                if nxt:
                    square(l, n, Q1)
                    guess_norm(l, n, 0)
                exps(l, b, 2)
                if nxt:
                    square(l, n, K1)
                copy_o(l, b, 0)
                if nxt:
                    copy_v(l, n, 1 - par, V0)
                exps(l, b, 3)
                if nxt:
                    copy_v(l, n, 1 - par, V1)
                    guess_norm(l, n, 1)
                    copy_qk(l, n, 1 - par, Q0)
                    copy_qk(l, n, 1 - par, K0)
                copy_o(l, b, 1)

            def ffn_gate(l, q, c):
                j = q * FCH + c
                act.wait_ge(f_h_ps, (l * NQ + q) * FCH + c + 1)
                if j >= 2:
                    act.wait_ge(f_h, (l * NQ + q) * FCH + c - 1)
                A(gate[:, j % 2, :], ps[0:FC, [4, 7][j % 2], :], ACT.Gelu, bias=vec[0:FC, 2 + FCH + c:3 + FCH + c]).then_inc(f_gate, 1)

            act.wait_ge(ld_const, 80)
            A(ident16[:], ident, ACT.Copy).then_inc(const_ready, 1)
            act.wait_ge(const_ready, 7)
            for q in range(NQ):
                cross_attention(q)
            with act.Fori(0, L) as l:
                copy_xt(l, 0, 0)
                copy_xt(l, 1, 1)
                square(l, 0, Q0)
                square(l, 0, K0)
                square(l, 0, Q1)
                guess_norm(l, 0, 0)
                square(l, 0, K1)
                copy_v(l, 0, 0, V0)
                copy_v(l, 0, 0, V1)
                guess_norm(l, 0, 1)
                copy_qk(l, 0, 0, Q0)
                copy_qk(l, 0, 0, K0)
                with act.Fori(0, PAIRS - 1) as j:
                    attention(l, 2 * j, 0)
                    attention(l, 2 * j + 1, 1)
                attention(l, B - 2, 0, nxt2=False)
                attention(l, B - 1, 1, nxt=False, nxt2=False)
                act.wait_ge(ld_ffn, 64 * l + 64)
                for q in range(NQ):
                    for c in range(FCH):
                        ffn_gate(l, q, c)

        @block.gpsimd
        def _(pool):
            G = nc.gpsimd
            nt_count = [0]

            G.memset(ones[:], 1.0).then_inc(const_ready, 1)
            G.memset(minus_half[:], -0.5).then_inc(const_ready, 1)
            G.memset(three_halves[:], 1.5).then_inc(const_ready, 1)
            G.memset(half_shift[:], 0.5 * float(np.log(LN_SHIFT))).then_inc(const_ready, 1)

            def power(src, dst, steps, at):
                G.tensor_scalar(dst, src, EPS, None, ALU.add).then_inc(steps, 1)
                pool.wait_ge(steps, at)
                return G.tensor_tensor(dst, dst, minus_half[:], ALU.pow)

            pool.wait_ge(const_ready, 7)
            for n in range(2 * NQ):
                pool.wait_ge(c_var, n + 1)
                power(mv[:, n % 2, :, 1], rstd[:, n % 2, :], f_pow, n + 1).then_inc(c_rstd, 1)

            def copy_x(l, b, par, first=False):
                if not first:
                    wait_apart(pool, xt_ps, count(l, b, 1, -1))
                G.tensor_copy(xs[:, par, :], xr[:, b:b + 1, :] if isinstance(b, int) else xr[:, bass.ds(b, 1), :]).then_inc(xs_ready, 1)

            def rotate(l, b, c):
                pool.wait_ge(rope_done, count(l, b, 4, c + 1))
                G.tensor_tensor(t1[:, c, :], t1[:, c, :], t2[:, c, :], ALU.add).then_inc(qk_added, 1)

            def refine_norm(l, b, u):
                pool.wait_ge(rn_guess, count(l, b, 2, u + 1))
                r = rn[:, u].rearrange("p a h -> p (a h)")
                s = ss[:, u].rearrange("p a h -> p (a h)")
                t = nt[:, u, :]
                base = count(l, b, 8, 4 * u)
                G.tensor_tensor(t, r, r, ALU.mult).then_inc(newton, 1)
                pool.wait_ge(newton, base + 1)
                G.tensor_tensor(t, t, s, ALU.mult).then_inc(newton, 1)
                pool.wait_ge(newton, base + 2)
                G.tensor_tensor(t, t, three_halves[:], ALU.add).then_inc(newton, 1)
                pool.wait_ge(newton, base + 3)
                G.tensor_tensor(r, r, t, ALU.mult).then_inc(newton, 1)

            def normalise(l, b, c):
                u = c // 2
                pool.wait_ge(newton, count(l, b, 8, 4 * u + 4))
                pool.wait_ge(qk_added, count(l, b, 4, c + 1))
                w = t1[:, c, :].rearrange("p (h e) -> p h e", h=8)
                G.tensor_tensor(w, w, rn[:, u, c % 2, :].unsqueeze(2).broadcast_to([P, 8, E]), ALU.mult).then_inc(qk_ready, 1)

            def normalise_p(l, b, g):
                pool.wait_ge(rsum_ready, count(l, b, 4, g + 1))
                w = pr[:, g % 2]
                G.tensor_tensor(w, w, rsum[:, g, :].unsqueeze(2).broadcast_to([P, 4, P]), ALU.mult).then_inc(pr_ready, 1)

            def attention(l, b, par, nxt=True, nxt2=True):
                n = b + 1
                normalise(l, b, Q1)
                normalise(l, b, K1)
                if nxt2:
                    copy_x(l, b + 2, par)
                normalise_p(l, b, 0)
                if nxt:
                    rotate(l, n, Q0)
                normalise_p(l, b, 1)
                if nxt:
                    rotate(l, n, K0)
                    refine_norm(l, n, 0)
                    normalise(l, n, Q0)
                normalise_p(l, b, 2)
                if nxt:
                    normalise(l, n, K0)
                    rotate(l, n, Q1)
                normalise_p(l, b, 3)
                if nxt:
                    rotate(l, n, K1)
                    refine_norm(l, n, 1)

            with pool.Fori(0, L) as l:
                wait_apart(pool, x_final, (l + 1) * NQ)
                copy_x(l, 0, 0, first=True)
                copy_x(l, 1, 1, first=True)
                rotate(l, 0, Q0)
                rotate(l, 0, K0)
                refine_norm(l, 0, 0)
                normalise(l, 0, Q0)
                normalise(l, 0, K0)
                rotate(l, 0, Q1)
                rotate(l, 0, K1)
                refine_norm(l, 0, 1)
                with pool.Fori(0, PAIRS - 1) as j:
                    attention(l, 2 * j, 0)
                    attention(l, 2 * j + 1, 1)
                attention(l, B - 2, 0, nxt2=False)
                attention(l, B - 1, 1, nxt=False, nxt2=False)
                for q in range(NQ):
                    wait_apart(pool, f_var, l * NQ + q + 1)
                    power(mv[:, q % 2, :, 1], rstd[:, q % 2, :], f_pow, (l + 2) * NQ + q + 1).then_inc(f_rstd, 1)

        @block.vector
        def _(dve):
            V = nc.vector

            V.memset(ss[:], 0.0).then_inc(x_updated, 1)
            V.memset(xt[E:P, :, 0:1], 0.0).then_inc(const_ready, 1)
            dve.wait_ge(ld_const, 80)
            V.tensor_copy(band16[:], consts[:, 0:P].unsqueeze(1).broadcast_to([P, 4, P])).then_inc(const_ready, 1)

            def stats(src, n):
                for b in range(QUAD):
                    V.bn_stats(st[:, n % 2, b, :], src(b)).then_inc(c_stats, 1)

            def aggregate(n, total, done):
                wait_apart(dve, c_stats, total)
                for b in range(QUAD):
                    i = V.bn_aggr(mv[:, n % 2, b, :], st[:, n % 2, b, :])
                i.then_inc(done, 1)

            def apply(dst, src, n):
                for b in range(QUAD):
                    i = V.tensor_scalar(dst(b), src(b), mv[:, n % 2, b, 0:1], rstd[:, n % 2, b:b + 1], ALU.subtract, ALU.mult)
                return i

            def cross_attention(q):
                s = slice(q * QUAD, (q + 1) * QUAD)
                dve.wait_ge(ld_x[q], 16)
                stats(lambda b: x1[:, q * QUAD + b, :], 2 * q)
                aggregate(2 * q, 4 * (2 * q + 1), c_var)
                dve.wait_ge(c_rstd, 2 * q + 1)
                apply(lambda b: xh[:, b, :], lambda b: x1[:, q * QUAD + b, :], 2 * q).then_inc(c_xn, 1)
                dve.wait_ge(c_s_ps, q + 1)
                V.tensor_reduce(nmax[:, 0, :], ps[:, 5, :].rearrange("p (b k) -> p b k", b=QUAD)[:, :, 0:CT], AX.X, ALU.max,
                                negate=True).then_inc(c_max, 1)
                dve.wait_ge(c_max, 2 * q + 1)
                V.tensor_scalar(nmax[:, 1, :], nmax[:, 0, :], float(P) ** -0.5, None, ALU.mult).then_inc(c_max, 1)
                dve.wait_ge(c_exp, 4 * q + 4)
                V.reciprocal(rsum[:, 0, :], psums[:, 0, :]).then_inc(c_sum, 1)
                dve.wait_ge(c_sum, q + 1)
                V.tensor_tensor(pr[:, 0, :, 0:CT], pr[:, 0, :, 0:CT], rsum[:, 0, :].unsqueeze(2).broadcast_to([P, QUAD, CT]),
                                ALU.mult).then_inc(c_pn, 1)
                dve.wait_ge(c_o_ps, q + 1)
                V.tensor_tensor(x1[:, s, :], x1[:, s, :], ps[:, 7, :].rearrange("p (b d) -> p b d", b=QUAD), ALU.add).then_inc(c_x1, 1)
                dve.wait_ge(c_x1, q + 1)
                stats(lambda b: x1[:, q * QUAD + b, :], 2 * q + 1)
                aggregate(2 * q + 1, 4 * (2 * q + 2), c_var)
                dve.wait_ge(c_rstd, 2 * q + 2)
                apply(lambda b: xr[:, q * QUAD + b, :], lambda b: x1[:, q * QUAD + b, :], 2 * q + 1).then_inc(x_final, 1)

            def rope_tables(l):
                dve.wait_ge(ld_qkv, 32 * l + 32)
                for a in range(2):
                    V.tensor_tensor(rope[:, 2 * a, :], rope_base[:, 2 * a, :], qks[:, a, :], ALU.mult).then_inc(rope_ready, 1)
                    halves = lambda t: t.rearrange("p (a e) -> p a e", a=2)
                    V.tensor_tensor(halves(rope[:, 2 * a + 1, :]), halves(rope_base[:, 2 * a + 1, :]), halves(qks[:, a, :])[:, ::-1, :],
                                    ALU.mult).then_inc(rope_ready, 1)
                dve.wait_ge(rope_ready, 4 * l + 4)

            def rotary(l, b, c, first=False):
                dve.wait_ge(sq_ready, count(l, b, 4, c + 1))
                if not first:
                    dve.wait_ge(tq_ps, count(l, b, 4, c - 3))
                V.tensor_reduce(ss[:, c // 2, c % 2, :], sq[:, c % 2, :].rearrange("p (h e) -> p h e", h=8), AX.X, ALU.add).then_inc(ss_ready, 1)
                bank = ps[:, QKV_BANK[c % 3], :]
                a = c % 2
                cos = rope[:, 2 * a, :].unsqueeze(1).broadcast_to([P, 8, E])
                V.tensor_tensor(t1[:, c, :].rearrange("p (h e) -> p h e", h=8), bank.rearrange("p (h e) -> p h e", h=8), cos, ALU.mult)
                sin = rope[:, 2 * a + 1, :].rearrange("p (a e) -> p a e", a=2).unsqueeze(1).broadcast_to([P, 8, 2, E // 2])
                V.tensor_tensor(t2[:, c, :].rearrange("p (h a e) -> p h a e", h=8, a=2),
                                bank.rearrange("p (h a e) -> p h a e", h=8, a=2)[:, :, ::-1, :], sin, ALU.mult).then_inc(rope_done, 1)
                if c % 2:
                    dve.wait_ge(ss_ready, count(l, b, 4, c + 1))
                    w = ss[:, c // 2].rearrange("p a h -> p (a h)")
                    V.tensor_scalar(w, w, 1e-24, -0.5, ALU.max, ALU.mult).then_inc(ss_clamped, 1)

            def row_max(l, b, g):
                dve.wait_ge(s_ps, count(l, b, 4, g + 1))
                V.tensor_reduce(nmax[:, g, :], ps[:, S_BANK[g % 2], :].rearrange("p (h k) -> p h k", h=4), AX.X, ALU.max,
                                negate=True).then_inc(max_ready, 1)

            def inverse_sum(l, b, g):
                dve.wait_ge(exp_ready, count(l, b, 4, g + 1))
                V.reciprocal(rsum[:, g, :], psums[:, g, :]).then_inc(rsum_ready, 1)

            def copy_pT(l, b, g):
                dve.wait_ge(pt_ps, count(l, b, 4, g + 1))
                V.tensor_copy(pT[:, g].rearrange("p a q -> p (a q)"), ps[:, T_BANK[g % 2], :]).then_inc(pt_ready, 1)

            def add_residual(l, b):
                dve.wait_ge(y_ps, count(l, b, 1, 1))
                w = xr[:, b:b + 1, :] if isinstance(b, int) else xr[:, bass.ds(b, 1), :]
                V.tensor_tensor(w, w, ps[:, O_BANK, 0:P].unsqueeze(1), ALU.add).then_inc(x_updated, 1)

            def attention(l, b, par, nxt=True):
                n = b + 1
                row_max(l, b, 0)
                row_max(l, b, 1)
                inverse_sum(l, b, 0)
                if nxt:
                    rotary(l, n, Q0)
                inverse_sum(l, b, 1)
                if nxt:
                    rotary(l, n, K0)
                copy_pT(l, b, 0)
                if nxt:
                    rotary(l, n, Q1)
                row_max(l, b, 2)
                copy_pT(l, b, 1)
                if nxt:
                    rotary(l, n, K1)
                inverse_sum(l, b, 2)
                row_max(l, b, 3)
                copy_pT(l, b, 2)
                inverse_sum(l, b, 3)
                copy_pT(l, b, 3)
                add_residual(l, b)

            def ffn_stats(l, q):
                dve.wait_ge(f_shift_ps, l * NQ + q + 1)
                stats(lambda b: ps[:, q % 2, b * P:(b + 1) * P], q)
                aggregate(q, 8 * NQ + 4 * (l * NQ + q + 1), f_var)

            def ffn_normalise(l, q):
                dve.wait_ge(f_rstd, l * NQ + q + 1)
                if q >= 1:
                    dve.wait_ge(f_xhT_ps, l * NQ + q)
                apply(lambda b: xh[:, b, :], lambda b: ps[:, q % 2, b * P:(b + 1) * P], q).then_inc(f_xh, 1)

            def ffn_affine(l, q):
                dve.wait_ge(f_xhT_ps, l * NQ + q + 1)
                V.tensor_scalar(xhT[:, q % 2, :], ps[:, 5, :], vec[:, 0:1], vec[:, 1:2], ALU.mult, ALU.add).then_inc(f_xhT, 1)

            def ffn_gated(l, q, c):
                j = q * FCH + c
                dve.wait_ge(f_gate, (l * NQ + q) * FCH + c + 1)
                V.scalar_tensor_tensor(out=hT[:, q % 2, c, :], in0=ps[0:FC, 2 + j % 2, :], scalar=vec[0:FC, 2 + c:3 + c],
                                       in1=gate[:, j % 2, :], op0=ALU.add, op1=ALU.mult).then_inc(f_h, 1)

            def ffn_residual(l, q):
                dve.wait_ge(f_y_ps, l * NQ + q + 1)
                w = xr[:, q * QUAD:(q + 1) * QUAD, :]
                V.tensor_tensor(w, w, ps[:, 6, :].rearrange("p (b d) -> p b d", b=QUAD), ALU.add).then_inc(x_final, 1)

            dve.wait_ge(const_ready, 7)
            for q in range(NQ):
                cross_attention(q)
            with dve.Fori(0, L) as l:
                rope_tables(l)
                rotary(l, 0, Q0, first=True)
                rotary(l, 0, K0, first=True)
                rotary(l, 0, Q1, first=True)
                rotary(l, 0, K1, first=True)
                with dve.Fori(0, PAIRS - 1) as j:
                    attention(l, 2 * j, 0)
                    attention(l, 2 * j + 1, 1)
                attention(l, B - 2, 0)
                attention(l, B - 1, 1, nxt=False)
                dve.wait_ge(ld_ffn, 64 * l + 64)
                ffn_stats(l, 0)
                ffn_stats(l, 1)
                ffn_normalise(l, 0)
                ffn_affine(l, 0)
                for q in range(NQ + 1):
                    if q < NQ:
                        if q + 1 < NQ:
                            ffn_normalise(l, q + 1)
                        ffn_gated(l, q, 0)
                    if q >= 1:
                        ffn_residual(l, q - 1)
                    if q < NQ:
                        ffn_gated(l, q, 1)
                        if q + 1 < NQ:
                            ffn_gated(l, q, 2)
                            ffn_affine(l, q + 1)
                        else:
                            ffn_gated(l, q, 2)
                        if q + 2 < NQ:
                            ffn_stats(l, q + 2)
            for q in range(NQ):
                s = slice(q * QUAD, (q + 1) * QUAD)
                if q == 0:
                    dve.wait_ge(x_final, (L + 1) * NQ)
                V.tensor_tensor(x1[:, s, :], x1[:, s, :], xr[:, s, :], ALU.add).then_inc(final_sum, 1)


def kernel(**inputs):
    import concourse.bacc as bacc
    from concourse.bass_utils import run_bass_kernel_spmd

    a = {k: np.ascontiguousarray(np.asarray(w)) for k, w in inputs.items()}
    w1 = np.zeros((L, P, 2, FCH * FC), np.float32)
    w1[:, :, :, :FI] = a["L0_ffn_W1"].reshape(L, P, 2, FI)
    b1 = np.zeros((L, 2, FCH * FC), np.float32)
    b1[:, :, :FI] = a["L0_ffn_b1"].reshape(L, 2, FI)
    w2 = np.zeros((L, FCH * FC, P), np.float32)
    w2[:, :FI] = a["L0_ffn_W2"]
    vec = np.zeros((L, P, 2 + 2 * FCH), np.float32)
    vec[:, :, 0] = a["L0_ffn_ln_g"]
    vec[:, :, 1] = a["L0_ffn_ln_b"]
    vec[:, :FC, 2:] = b1.reshape(L, 2 * FCH, FC).transpose(0, 2, 1)
    rope, const = constants()
    arrays = {
        "x_in": a["x"],
        "ctx_in": a["ctx_1024"],
        "xw_in": np.stack([a["L0_xattn_Wq"], a["L0_xattn_Wk"], a["L0_xattn_Wv"]], 1),
        "xv_in": np.stack([a["L0_xattn_bq"], a["L0_xattn_bk"]], 1),
        "bv_in": a["L0_xattn_bv"].reshape(1, P),
        "wqkv_in": a["L0_ffn_Wqkv"],
        "qk_scale_in": np.stack([a["L0_ffn_q_scale"], a["L0_ffn_k_scale"]], 1),
        "wo_in": a["L0_ffn_Wo"].reshape(L, 8, P, P).transpose(0, 2, 1, 3),
        "w1_in": w1.reshape(L, P, 2 * FCH, FC),
        "w2_in": w2.reshape(L, FCH, FC, P).transpose(0, 2, 1, 3),
        "vec_in": vec,
        "b2_in": a["L0_ffn_b2"].reshape(L, 1, P),
        "rope_in": rope,
        "const_in": const,
    }
    arrays = {k: np.ascontiguousarray(w) for k, w in arrays.items()}
    nc = bacc.Bacc("TRN2", target_bir_lowering=False, num_devices=1)
    args = [nc.dram_tensor(k, w.shape, F32, kind="ExternalInput").ap() for k, w in arrays.items()]
    out = nc.dram_tensor("out", (B, P, P), F32, kind="ExternalOutput").ap()
    build(nc, *args, out)
    r = run_bass_kernel_spmd(nc, [arrays], core_ids=[0])
    return r.results[0]["out"]
```

```python
import numpy as np
import concourse.bass as bass
from concourse import mybir
from concourse.alu_op_type import AluOpType as ALU

F32 = mybir.dt.float32
BF16 = mybir.dt.bfloat16
F32R = mybir.dt.float32r
ACT = mybir.ActivationFunctionType
AX = mybir.AxisListType

P = 128
B = 16
CT = 120
L = 6
H = 16
E = 64
WIN = 32
INNER = H * E
FI = 341
FCH = 3
FC = 114
QUAD = 4
NQ = B // QUAD
EPS = 1e-5
QK_SCALE = 8.0
MASKED = -1e25
LN_SHIFT = 2.0 ** 20

CHUNK_COLS = [0, INNER, 512, INNER + 512, 2 * INNER, 2 * INNER + 512]
Q0, K0, Q1, K1, V0, V1 = range(6)


def head(g, k):
    return 8 * (g // 2) + 2 * k + g % 2


def constants():
    half = np.arange(0, E, 2, dtype=np.float32)
    inv_freq = (np.float32(1.0) / np.power(np.float32(10000.0), half / np.float32(E))).astype(np.float32)
    t = np.arange(P, dtype=np.float32)
    fr = (t[:, None] * inv_freq[None, :]).astype(np.float32)
    fr = np.concatenate([fr, fr], -1)
    base = ((half + np.float32(0.4 * E)) / np.float32(1.4 * E)).astype(np.float32)
    power = ((t - P // 2) / np.float32(WIN // 2)).astype(np.float32)
    sc = np.power(base[None, :], power[:, None]).astype(np.float32)
    sc = np.concatenate([sc, sc], -1)
    cos, sin = np.cos(fr).astype(np.float32), np.sin(fr).astype(np.float32)
    sign = np.where(np.arange(E) < E // 2, -1.0, 1.0).astype(np.float32)
    inv = (np.float32(1.0) / sc).astype(np.float32)
    rope = np.stack([cos * sc * QK_SCALE, sin * sc * sign * QK_SCALE, cos * inv, sin * inv * sign], 1)
    q, k = np.arange(P)[:, None], np.arange(P)[None, :]
    band = np.where((k <= q) & (q <= k + WIN), 0.0, MASKED).astype(np.float32)
    ident = np.eye(P, dtype=np.float32)
    shift = np.eye(P, k=1, dtype=np.float32)
    return rope.astype(np.float32), np.concatenate([band, ident, shift], 1)


def build(nc, x_d, ctx_d, xw_d, xv_d, bv_d, wqkv_d, qk_scale_d, wo_d, w1_d, w2_d, vec_d, b2_d, rope_d, const_d, out_d):
    def sb(name, shape, dt=F32):
        return nc.alloc_sbuf_tensor(name, shape, dt)

    x1 = sb("x1", [P, B, P])
    xr = sb("xr", [P, B, P])
    wqkv = sb("wqkv", [P, 3 * INNER])
    w_hi = sb("w_hi", [P, 3 * INNER], F32R)
    w_lo = sb("w_lo", [P, 3 * INNER], F32R)
    wo = sb("wo", [P, 8, P])
    w1 = sb("w1", [P, 2 * FCH, FC])
    w2 = sb("w2", [FC, FCH, P])
    vec = sb("vec", [P, 2 + 2 * FCH])
    b2 = sb("b2", [1, P])
    qks = sb("qks", [P, 2, E])
    rope_base = sb("rope_base", [P, 4, E])
    rope = sb("rope", [P, 4, E])
    consts = sb("consts", [P, 3 * P])
    ident = consts[:, P:2 * P]
    shift = consts[:, 2 * P:3 * P]
    ident16 = sb("ident16", [P, P], BF16)
    band16 = sb("band16", [P, 4, P], BF16)
    ones = sb("ones", [1, P])
    zeros = sb("zeros", [P, 2])
    half_shift = sb("half_shift", [P, 1])
    three_halves = sb("three_halves", [P, 16])
    minus_half = sb("minus_half", [P, QUAD])
    xs = sb("xs", [P, 2, P])
    xt_hi = sb("xt_hi", [P, 2, P], F32R)
    xt_lo = sb("xt_lo", [P, 2, P], F32R)
    sq = sb("sq", [P, 4, 512])
    ss = sb("ss", [P, 2, 2, 2, 8])
    rn = sb("rn", [P, 2, 2, 2, 8])
    nt = sb("nt", [P, 2, 16])
    t1 = sb("t1", [P, 4, 512])
    t2 = sb("t2", [P, 4, 512])
    qT = sb("qT", [P, 2, 8, P])
    kT = sb("kT", [P, 2, 8, P])
    v = sb("v", [P, 2, INNER])
    nmax = sb("nmax", [P, 4, 4])
    nbias = sb("nbias", [P, 4, 4])
    psums = sb("psums", [P, 4, 4])
    rsum = sb("rsum", [P, 4, 4])
    pr = sb("pr", [P, 4, 4, P])
    pT = sb("pT", [P, 4, 4, P])
    oT = sb("oT", [P, 2, 8, P])
    st = sb("st", [P, 2, QUAD, 6])
    mv = sb("mv", [P, 2, QUAD, 2])
    rstd = sb("rstd", [P, 2, QUAD])
    xh = sb("xh", [P, QUAD, P])
    xhT = sb("xhT", [P, 2, QUAD * P])
    gate = sb("gate", [FC, 2, QUAD * P])
    hT = sb("hT", [FC, 2, FCH, QUAD * P])
    xw = sb("xw", [P, 3, P])
    xvec = sb("xvec", [P, 2])
    bv = sb("bv", [1, P])
    ctx = sb("ctx", [CT, 2, QUAD, P])
    ctxT = sb("ctxT", [P, QUAD * CT])
    xq = sb("xq", [P, QUAD * P])
    xk = sb("xk", [P, QUAD * CT])
    xvv = sb("xvv", [CT, QUAD, P])

    ps = nc.alloc_psum_tensor("ps", [P, 8, 512], F32)
    X_BANK, Y_BANK = 6, 7
    QKV_BANK = [1, 0, 1, 0, 0, 1]
    TQ_BANK = [4, 4, 5, 4]
    S_BANK = [2, 3, 2, 3]
    TP_BANK = [4, 5, 5, 5]
    O_BANK = [7, 6]
    def sem(name):
        return nc.alloc_semaphore(name)

    ld_const, ld_qkv, ld_scale, ld_wo, ld_ffn = (sem(s) for s in ("ld_const", "ld_qkv", "ld_scale", "ld_wo", "ld_ffn"))
    ld_x = [sem(f"ld_x{q}") for q in range(NQ)]
    ld_ctx = [sem(f"ld_ctx{q}") for q in range(2)]
    const_ready, x_final = sem("const_ready"), sem("x_final")
    rope_ready = sem("rope_ready")
    zeroed, w_hi_ready, w_ready = sem("zeroed"), sem("w_hi_ready"), sem("w_ready")

    def sems(name, n):
        return [sem(f"{name}{k}") for k in range(n)]

    xs_ready, xt_ps, xt_hi_ready, xt_ready = (sem(s) for s in ("xs_ready", "xt_ps", "xt_hi_ready", "xt_ready"))
    qkv_ps = sems("qkv_ps", 6)
    sq_ready, ss_ready, rope_done, qk_added, tq_ps, tq_ready = (
        sems(s, 4) for s in ("sq_ready", "ss_ready", "rope_done", "qk_added", "tq_ps", "tq_ready"))
    ss_clamped, ln_done, rn_guess, rn_ready, k_ready, v_ready = (
        sems(s, 2) for s in ("ss_clamped", "ln_done", "rn_guess", "rn_ready", "k_ready", "v_ready"))
    s_ps, max_ready, bias_ready, exp_ready, rsum_ready, pr_ready, pt_ps, pt_ready = (
        sems(s, 4) for s in ("s_ps", "max_ready", "bias_ready", "exp_ready", "rsum_ready", "pr_ready", "pt_ps", "pt_ready"))
    o_ps, o_ready = sems("o_ps", 2), sems("o_ready", 2)
    y_ps, x_updated = sem("y_ps"), sem("x_updated")
    newton = sems("newton", 2)
    f_shift_ps, f_stats, f_var, f_pow, f_rstd, f_xh, f_xhT_ps, f_xhT, f_h_ps, f_gate, f_h, f_y_ps = (
        sem("f_" + s) for s in ("shift_ps", "stats", "var", "pow", "rstd", "xh", "xhT_ps", "xhT", "h_ps", "gate", "h", "y_ps"))
    c_stats, c_var, c_rstd, c_xn, c_tr_ps, c_tr, c_qk_ps, c_qk, c_s_ps, c_max, c_exp, c_sum, c_pn, c_pT_ps, c_pT, c_o_ps, c_x1 = (
        sem("c_" + s) for s in ("stats", "var", "rstd", "xn", "tr_ps", "tr", "qk_ps", "qk", "s_ps", "max", "exp", "sum", "pn", "pT_ps", "pT", "o_ps", "x1"))
    final_sum, stored, passed = sem("final_sum"), sem("stored"), sem("passed")

    def nth(l, b, per=1, k=0):
        return l * (B * per) + (b + 1) * per + k

    STEPS = B + 2
    HEAD_STEPS, TAIL_STEPS = 4, 2

    def live(i, lag):
        return not isinstance(i, int) or 0 <= i - lag < B

    def run(l, i, parity, lag, task, *args):
        if live(i, lag):
            task(l, i - lag, (parity + lag) % 2, *args)

    def bank_free(eng, l, i, *users):
        for semaphore, lag in users:
            if live(i, lag):
                eng.wait_ge(semaphore, nth(l, i - lag))
                return

    def x_ahead(i):
        return isinstance(i, int) and i <= 1

    def last_step(i):
        return isinstance(i, int) and i == STEPS - 1

    def steps(eng, l, step):
        for i in range(1, HEAD_STEPS):
            step(l, i, i % 2)
        with eng.Fori(0, (STEPS - HEAD_STEPS - TAIL_STEPS) // 2) as j:
            step(l, 2 * j + HEAD_STEPS, 0)
            step(l, 2 * j + (HEAD_STEPS + 1), 1)
        for i in range(STEPS - TAIL_STEPS, STEPS):
            step(l, i, i % 2)

    def all_layers(eng, layer):
        with eng.Fori(0, L - 1) as l:
            layer(l, False)
        layer(L - 1, True)

    def wait_apart(eng, semaphore, value):
        eng.wait_ge(semaphore, value)
        eng.sem_inc(passed, 1)

    block = nc.Block()
    with block as block:

        @block.sync
        def _(sp):
            sp.dma_start(x1[:, 0:QUAD, :], x_d[0:QUAD].rearrange("b t d -> t b d")).then_inc(ld_x[0], 16)
            sp.dma_start(consts[:], const_d).then_inc(ld_const, 16)
            sp.dma_start(xw[:], xw_d).then_inc(ld_const, 16)
            sp.dma_start(xvec[:], xv_d).then_inc(ld_const, 16)
            sp.dma_start(bv[:], bv_d).then_inc(ld_const, 16)
            sp.dma_start(rope_base[:], rope_d).then_inc(ld_const, 16)
            for q in range(NQ):
                if q >= 2:
                    sp.wait_ge(c_tr_ps, 2 * (q - 2) + 2)
                sp.dma_start(ctx[:, q % 2], ctx_d[q * QUAD:(q + 1) * QUAD].rearrange("b t d -> t b d")).then_inc(ld_ctx[q % 2], 16)
                if q + 1 < NQ:
                    s = slice((q + 1) * QUAD, (q + 2) * QUAD)
                    sp.dma_start(x1[:, s, :], x_d[s].rearrange("b t d -> t b d")).then_inc(ld_x[q + 1], 16)

            def load_rest(l):
                sp.dma_start(w1[:], w1_d[l]).then_inc(ld_ffn, 16)
                sp.dma_start(w2[:], w2_d[l]).then_inc(ld_ffn, 16)
                sp.dma_start(vec[:], vec_d[l]).then_inc(ld_ffn, 16)
                sp.dma_start(b2[:], b2_d[l]).then_inc(ld_ffn, 16)

            def load_scales(l):
                sp.dma_start(qks[:], qk_scale_d[l].unsqueeze(0).broadcast_to([P, 2, E])).then_inc(ld_scale, 16)

            sp.dma_start(wqkv[:], wqkv_d[0]).then_inc(ld_qkv, 16)
            load_scales(0)
            sp.dma_start(wo[:], wo_d[0]).then_inc(ld_wo, 16)
            load_rest(0)
            with sp.Fori(1, L) as l:
                wait_apart(sp, w_ready, l * 6)
                sp.dma_start(wqkv[:], wqkv_d[l]).then_inc(ld_qkv, 16)
                wait_apart(sp, rope_ready, l * 4)
                load_scales(l)
                wait_apart(sp, y_ps, nth(l, -1))
                sp.dma_start(wo[:], wo_d[l]).then_inc(ld_wo, 16)
                wait_apart(sp, f_y_ps, l * NQ)
                wait_apart(sp, f_h, l * NQ * FCH)
                load_rest(l)
            for q in range(NQ):
                sp.wait_ge(final_sum, q + 1)
                s = slice(q * QUAD, (q + 1) * QUAD)
                sp.dma_start(out_d[s].rearrange("b t d -> t b d"), x1[:, s, :]).then_inc(stored, 16)
            sp.wait_ge(stored, 16 * NQ)

        @block.tensor
        def _(pe):
            mm, tr = nc.tensor.matmul, nc.tensor.transpose

            def cross_attention(q):
                pe.wait_ge(c_xn, q + 1)
                if q >= 1:
                    pe.wait_ge(c_x1, q)
                for b in range(QUAD):
                    i = tr(ps[:, 0, b * P:(b + 1) * P], xh[:, b, :], ident)
                i.then_inc(c_tr_ps, 1)
                pe.wait_ge(ld_ctx[q % 2], 16 * (q // 2 + 1))
                for b in range(QUAD):
                    i = tr(ps[:, 1, b * CT:(b + 1) * CT], ctx[:, q % 2, b, :], ident[0:CT, 0:CT])
                i.then_inc(c_tr_ps, 1)
                pe.wait_ge(c_tr, 2 * q + 1)
                mm(ps[:, 2, :], xw[:, 0, :], xhT[:, 0, :], start=True, stop=True).then_inc(c_qk_ps, 1)
                pe.wait_ge(c_tr, 2 * q + 2)
                mm(ps[:, 3, 0:QUAD * CT], xw[:, 1, :], ctxT[:], start=True, stop=True).then_inc(c_qk_ps, 1)
                for b in range(QUAD):
                    o = ps[0:CT, 4, b * P:(b + 1) * P]
                    mm(o, ctxT[:, b * CT:(b + 1) * CT], xw[:, 2, :], start=True, stop=False)
                    i = mm(o, ones[0:1, 0:CT], bv[:], start=False, stop=True)
                i.then_inc(c_qk_ps, 1)
                pe.wait_ge(c_qk, 3 * q + 2)
                for b in range(QUAD):
                    i = mm(ps[:, 5, b * P:b * P + CT], xq[:, b * P:(b + 1) * P], xk[:, b * CT:(b + 1) * CT], start=True, stop=True)
                i.then_inc(c_s_ps, 1)
                pe.wait_ge(c_pn, q + 1)
                for b in range(QUAD):
                    i = tr(ps[0:CT, 6, b * P:(b + 1) * P], pr[:, 0, b, 0:CT], ident)
                i.then_inc(c_pT_ps, 1)
                pe.wait_ge(c_pT, q + 1)
                pe.wait_ge(c_qk, 3 * q + 3)
                for b in range(QUAD):
                    i = mm(ps[:, 7, b * P:(b + 1) * P], pT[0:CT, 0, b, :], xvv[:, b, :], start=True, stop=True)
                i.then_inc(c_o_ps, 1)

            def transpose_x(l, b, par):
                pe.wait_ge(xs_ready, nth(l, b))
                tr(ps[:, X_BANK, 0:P], xs[:, par, :], ident).then_inc(xt_ps, 1)

            def project(l, b, par, c):
                if c == Q0:
                    pe.wait_ge(xt_ready, nth(l, b))
                if isinstance(b, int) and b == 0:
                    pe.wait_ge(w_ready, l * 6 + c + 1)
                w = slice(CHUNK_COLS[c], CHUNK_COLS[c] + 512)
                o = ps[:, QKV_BANK[c], :]
                mm(o, xt_hi[:, par, :], w_hi[:, w], start=True, stop=False)
                mm(o, xt_hi[:, par, :], w_lo[:, w], start=False, stop=False)
                mm(o, xt_lo[:, par, :], w_hi[:, w], start=False, stop=True).then_inc(qkv_ps[c], 1)

            def transpose_qk(l, b, par, c):
                pe.wait_ge(k_ready[c // 2] if c % 2 else qk_added[c], nth(l, b))
                for k in range(4):
                    i = tr(ps[:, TQ_BANK[c], k * P:(k + 1) * P], t1[:, c, k * P:(k + 1) * P], ident)
                i.then_inc(tq_ps[c], 1)

            def scores(l, b, par, g):
                u = g // 2
                pe.wait_ge(tq_ready[2 * u], nth(l, b))
                pe.wait_ge(tq_ready[2 * u + 1], nth(l, b))
                o = S_BANK[g]
                mm(ps[:, o, :], ident16[:], band16[:].rearrange("p a k -> p (a k)"), start=True, stop=False, skip_group_check=True)
                for k in range(4):
                    h = head(g, k)
                    r = slice(E * (h % 2), E * (h % 2) + E)
                    i = mm(ps[:, o, k * P:(k + 1) * P], qT[r, par, h // 2, :], kT[r, par, h // 2, :], start=False, stop=k == 3,
                           skip_group_check=True)
                i.then_inc(s_ps[g], 1)

            def transpose_p(l, b, par, g):
                pe.wait_ge(pr_ready[g], nth(l, b))
                for k in range(4):
                    i = tr(ps[:, TP_BANK[g], k * P:(k + 1) * P], pr[:, g, k, :], ident)
                i.then_inc(pt_ps[g], 1)

            def weigh_values(l, b, par, s):
                pe.wait_ge(pt_ready[2 * s], nth(l, b))
                pe.wait_ge(pt_ready[2 * s + 1], nth(l, b))
                pe.wait_ge(v_ready[s], nth(l, b))
                for k in range(4):
                    for odd in range(2):
                        g = 2 * s + odd
                        h = head(g, k)
                        i = mm(ps[odd * E:odd * E + E, O_BANK[s], k * P:(k + 1) * P], v[:, par, h * E:(h + 1) * E], pT[:, g, k, :],
                               start=True, stop=True)
                i.then_inc(o_ps[s], 1)

            def output_projection(l, b, par):
                pe.wait_ge(o_ready[0], nth(l, b))
                pe.wait_ge(o_ready[1], nth(l, b))
                for c in range(8):
                    i = mm(ps[:, Y_BANK, 0:P], oT[:, par, c, :], wo[:, c, :], start=c == 0, stop=c == 7)
                i.then_inc(y_ps, 1)

            def step(l, i, parity):
                if last_step(i):
                    ffn_shift(l, 0)
                if live(i, 1):
                    bank_free(pe, l, i, (tq_ready[K1], 2), (pt_ready[0], 3), (tq_ready[K0], 2), (tq_ready[Q0], 2))
                    transpose_qk(l, i - 1, 1 - parity, Q0)
                if live(i, 2):
                    bank_free(pe, l, i, (pt_ready[2], 3), (pt_ready[3], 3), (tq_ready[Q1], 2))
                    transpose_p(l, i - 2, parity, 1)
                if live(i, 2):
                    bank_free(pe, l, i, (exp_ready[0], 2))
                    scores(l, i - 2, parity, 2)
                if last_step(i):
                    ffn_shift(l, 1)
                if live(i, 0) and not x_ahead(i):
                    bank_free(pe, l, i, (o_ready[1], 3), (xt_ready, 1))
                    transpose_x(l, i, parity)
                if live(i, 1):
                    bank_free(pe, l, i, (rope_done[K1], 1))
                    project(l, i - 1, 1 - parity, V0)
                if live(i, 1):
                    bank_free(pe, l, i, (tq_ready[Q0], 1))
                    transpose_qk(l, i - 1, 1 - parity, K0)
                if live(i, 1):
                    bank_free(pe, l, i, (pt_ready[1], 2), (pt_ready[2], 3), (pt_ready[3], 3), (tq_ready[Q1], 2))
                    transpose_qk(l, i - 1, 1 - parity, Q1)
                if live(i, 0):
                    bank_free(pe, l, i, (v_ready[1], 2), (rope_done[Q1], 1), (rope_done[Q0], 1))
                    project(l, i, parity, Q0)
                if live(i, 0):
                    bank_free(pe, l, i, (v_ready[0], 1), (rope_done[K1], 1), (rope_done[K0], 1))
                    project(l, i, parity, K0)
                if live(i, 1):
                    bank_free(pe, l, i, (exp_ready[3], 2), (exp_ready[1], 2))
                    scores(l, i - 1, 1 - parity, 1)
                if live(i, 2):
                    bank_free(pe, l, i, (tq_ready[K0], 1), (tq_ready[Q0], 1), (tq_ready[K1], 2))
                    transpose_p(l, i - 2, parity, 0)
                if live(i, 2):
                    bank_free(pe, l, i, (tq_ready[Q1], 1), (pt_ready[1], 2))
                    transpose_p(l, i - 2, parity, 3)
                if live(i, 0):
                    bank_free(pe, l, i, (rope_done[Q0], 0))
                    project(l, i, parity, Q1)
                if live(i, 1):
                    bank_free(pe, l, i, (pt_ready[0], 2), (tq_ready[K0], 1))
                    transpose_qk(l, i - 1, 1 - parity, K1)
                if live(i, 2):
                    bank_free(pe, l, i, (x_updated, 3), (o_ready[0], 3))
                    weigh_values(l, i - 2, parity, 0)
                if last_step(i):
                    ffn_transpose(l, 0)
                if live(i, 2):
                    bank_free(pe, l, i, (pt_ready[3], 2))
                    transpose_p(l, i - 2, parity, 2)
                if last_step(i):
                    ffn_up(l, 0, 0)
                if live(i, 0):
                    bank_free(pe, l, i, (rope_done[K0], 0))
                    project(l, i, parity, K1)
                if live(i, 1):
                    bank_free(pe, l, i, (exp_ready[2], 2), (exp_ready[0], 2))
                    scores(l, i - 1, 1 - parity, 0)
                if live(i, 2):
                    bank_free(pe, l, i, (xt_ready, 0), (o_ready[1], 3))
                    weigh_values(l, i - 2, parity, 1)
                if live(i, 1):
                    bank_free(pe, l, i, (exp_ready[1], 1))
                    scores(l, i - 1, 1 - parity, 3)
                if live(i, 2):
                    bank_free(pe, l, i, (o_ready[0], 2))
                    output_projection(l, i - 2, parity)
                if live(i, 1):
                    bank_free(pe, l, i, (rope_done[Q1], 0), (rope_done[Q0], 0), (v_ready[1], 2))
                    project(l, i - 1, 1 - parity, V1)

            def ffn_shift(l, q):
                pe.wait_ge(x_updated, nth(l, QUAD * q + QUAD - 1))
                if q >= 2:
                    pe.wait_ge(f_xhT, l * NQ + q - 1)
                else:
                    pe.wait_ge(v_ready[q], nth(l, B - 1))
                s = slice(q * QUAD, (q + 1) * QUAD)
                o = ps[:, q % 2, :].rearrange("p (b d) -> p b d", b=QUAD)
                mm(o[:, :, 0:E], ident, xr[:, s, 0:E], start=True, stop=True)
                mm(o[:, :, E:P], shift, xr[:, s, E:P], start=True, stop=True).then_inc(f_shift_ps, 1)

            def ffn_transpose(l, q):
                pe.wait_ge(f_xh, l * NQ + q + 1)
                for b in range(QUAD):
                    i = tr(ps[:, q % 2, b * P:(b + 1) * P], xh[:, b, :], ident)
                i.then_inc(f_xhT_ps, 1)

            def ffn_up(l, q, c):
                j = q * FCH + c
                if c == 0:
                    if q == 0:
                        pe.wait_ge(ld_ffn, 64 * l + 64)
                    pe.wait_ge(f_xhT, l * NQ + q + 1)
                if j == 1:
                    pe.wait_ge(x_updated, nth(l, B - 1))
                if j >= 2:
                    pe.wait_ge(f_h, (l * NQ + q) * FCH + c - 1)
                mm(ps[0:FC, [4, 7][j % 2], :], w1[:, FCH + c, :], xhT[:, q % 2, :], start=True, stop=True)
                mm(ps[0:FC, 2 + j % 2, :], w1[:, c, :], xhT[:, q % 2, :], start=True, stop=True).then_inc(f_h_ps, 1)

            def ffn_down(l, q):
                pe.wait_ge(f_h, (l * NQ + q + 1) * FCH)
                if q >= 1:
                    pe.wait_ge(x_final, (l + 1) * NQ + q)
                for b in range(QUAD):
                    o = ps[:, 5, b * P:(b + 1) * P]
                    for c in range(FCH):
                        mm(o, hT[:, q % 2, c, b * P:(b + 1) * P], w2[:, c, :], start=c == 0, stop=False)
                    i = mm(o, ones[:], b2[:], start=False, stop=True)
                i.then_inc(f_y_ps, 1)

            pe.wait_ge(ld_const, 80)
            pe.wait_ge(const_ready, 8)
            for q in range(NQ):
                cross_attention(q)
            def layer(l, last):
                n = l + 1
                pe.wait_ge(x_final, n * NQ)
                pe.wait_ge(ld_wo, 16 * n)
                steps(pe, l, step)
                for q in range(NQ + 1):
                    if q == 2 and not last:
                        transpose_x(n, 0, 0)
                    if q == 3 and not last:
                        pe.wait_ge(xt_ready, nth(n, 0))
                        transpose_x(n, 1, 1)
                        project(n, 0, 0, K0)
                    if 1 <= q < NQ:
                        ffn_up(l, q, 0)
                    if q == 3 and not last:
                        project(n, 0, 0, Q0)
                    if q == NQ and not last:
                        pe.wait_ge(rope_done[Q0], nth(n, 0))
                        project(n, 0, 0, Q1)
                        pe.wait_ge(rope_done[K0], nth(n, 0))
                        project(n, 0, 0, K1)
                    if q >= 1:
                        ffn_down(l, q - 1)
                    if q < NQ:
                        ffn_up(l, q, 1)
                        if q + 1 < NQ:
                            ffn_transpose(l, q + 1)
                        ffn_up(l, q, 2)
                    if q + 2 < NQ:
                        ffn_shift(l, q + 2)

            pe.wait_ge(x_final, NQ)
            transpose_x(0, 0, 0)
            pe.wait_ge(xt_ready, 1)
            transpose_x(0, 1, 1)
            step(0, 0, 0)
            all_layers(pe, layer)

        @block.scalar
        def _(act):
            A = nc.scalar.activation

            def cross_attention(q):
                act.wait_ge(c_tr_ps, 2 * q + 1)
                A(xhT[:, 0, :], ps[:, 0, :], ACT.Copy).then_inc(c_tr, 1)
                act.wait_ge(c_tr_ps, 2 * q + 2)
                A(ctxT[:], ps[:, 1, 0:QUAD * CT], ACT.Copy).then_inc(c_tr, 1)
                act.wait_ge(c_qk_ps, 3 * q + 1)
                A(xq[:], ps[:, 2, :], ACT.Identity, bias=xvec[:, 0:1]).then_inc(c_qk, 1)
                act.wait_ge(c_qk_ps, 3 * q + 2)
                A(xk[:], ps[:, 3, 0:QUAD * CT], ACT.Identity, bias=xvec[:, 1:2]).then_inc(c_qk, 1)
                act.wait_ge(c_qk_ps, 3 * q + 3)
                A(xvv[:].rearrange("p b d -> p (b d)"), ps[0:CT, 4, :], ACT.Copy).then_inc(c_qk, 1)
                act.wait_ge(c_max, 2 * q + 2)
                for b in range(QUAD):
                    A(pr[:, 0, b, 0:CT], ps[:, 5, b * P:b * P + CT], ACT.Exp, bias=nmax[:, 1, b:b + 1],
                      scale=float(P) ** -0.5, accum_out=psums[:, 0, b:b + 1]).then_inc(c_exp, 1)
                act.wait_ge(c_pT_ps, q + 1)
                A(pT[0:CT, 0].rearrange("p b d -> p (b d)"), ps[0:CT, 6, :], ACT.Copy).then_inc(c_pT, 1)

            def copy_xt(l, b, par):
                act.wait_ge(xt_ps, nth(l, b))
                A(xt_hi[0:E, par, :], ps[0:E, X_BANK, 0:P], ACT.Copy)
                A(xt_hi[E:P, par, 1:P], ps[E:P, X_BANK, 0:P - 1], ACT.Copy).then_inc(xt_hi_ready, 1)

            def square(l, b, par, c):
                act.wait_ge(qkv_ps[c], nth(l, b))
                A(sq[:, c, :], ps[:, QKV_BANK[c], :], ACT.Square).then_inc(sq_ready[c], 1)

            def guess_norm(l, b, par, u):
                act.wait_ge(ss_clamped[u], nth(l, b))
                r = rn[:, par, u].rearrange("p a h -> p (a h)")
                A(r, ss[:, par, u].rearrange("p a h -> p (a h)"), ACT.Ln, scale=-2.0 * LN_SHIFT).then_inc(ln_done[u], 1)
                act.wait_ge(ln_done[u], nth(l, b))
                A(r, r, ACT.Exp, scale=-0.5, bias=half_shift[:, 0:1]).then_inc(rn_guess[u], 1)

            def copy_v(l, b, par, s):
                act.wait_ge(qkv_ps[V0 + s], nth(l, b))
                A(v[:, par, s * 512:(s + 1) * 512], ps[:, QKV_BANK[V0 + s], :], ACT.Copy).then_inc(v_ready[s], 1)

            def copy_qk(l, b, par, c):
                act.wait_ge(tq_ps[c], nth(l, b))
                dst = (qT, kT)[c % 2]
                A(dst[:, par, 4 * (c // 2):4 * (c // 2) + 4, :].rearrange("p a t -> p (a t)"), ps[:, TQ_BANK[c], :],
                  ACT.Copy).then_inc(tq_ready[c], 1)

            def exps(l, b, par, g):
                act.wait_ge(bias_ready[g], nth(l, b))
                for k in range(4):
                    i = A(pr[:, g, k, :], ps[:, S_BANK[g], k * P:(k + 1) * P], ACT.Exp, bias=nbias[:, g, k:k + 1],
                          scale=rn[:, par, g // 2, 0, 2 * k + g % 2:2 * k + g % 2 + 1], accum_out=psums[:, g, k:k + 1])
                i.then_inc(exp_ready[g], 1)

            def copy_pT(l, b, par, g):
                act.wait_ge(pt_ps[g], nth(l, b))
                A(pT[:, g].rearrange("p a q -> p (a q)"), ps[:, TP_BANK[g], :], ACT.Copy).then_inc(pt_ready[g], 1)

            def copy_o(l, b, par, s):
                act.wait_ge(o_ps[s], nth(l, b))
                A(oT[:, par, 4 * s:4 * s + 4, :].rearrange("p a t -> p (a t)"), ps[:, O_BANK[s], :], ACT.Copy).then_inc(o_ready[s], 1)

            def step(l, i, parity):
                run(l, i, parity, 1, copy_qk, Q0)
                run(l, i, parity, 2, copy_pT, 1)
                if not x_ahead(i):
                    run(l, i, parity, 0, copy_xt)
                run(l, i, parity, 2, copy_v, 1)
                run(l, i, parity, 1, guess_norm, 1)
                run(l, i, parity, 1, copy_qk, K0)
                run(l, i, parity, 0, square, Q0)
                run(l, i, parity, 2, exps, 2)
                if last_step(i):
                    nc.scalar.preload_act_table(ACT.Gelu)
                run(l, i, parity, 0, square, K0)
                run(l, i, parity, 2, copy_pT, 3)
                run(l, i, parity, 0, square, Q1)
                run(l, i, parity, 1, exps, 1)
                run(l, i, parity, 1, copy_qk, K1)
                run(l, i, parity, 2, copy_pT, 2)
                run(l, i, parity, 2, copy_o, 0)
                run(l, i, parity, 1, exps, 0)
                run(l, i, parity, 0, guess_norm, 0)
                run(l, i, parity, 0, square, K1)
                run(l, i, parity, 1, exps, 3)

            def ffn_gate(l, q, c):
                j = q * FCH + c
                act.wait_ge(f_h_ps, (l * NQ + q) * FCH + c + 1)
                if j >= 2:
                    act.wait_ge(f_h, (l * NQ + q) * FCH + c - 1)
                A(gate[:, j % 2, :], ps[0:FC, [4, 7][j % 2], :], ACT.Gelu, bias=vec[0:FC, 2 + FCH + c:3 + FCH + c]).then_inc(f_gate, 1)

            act.wait_ge(ld_const, 80)
            A(ident16[:], ident, ACT.Copy).then_inc(const_ready, 1)
            act.wait_ge(const_ready, 8)
            for q in range(NQ):
                cross_attention(q)
            def layer(l, last):
                n = l + 1
                steps(act, l, step)
                act.wait_ge(ld_ffn, 64 * n)
                for q in range(NQ):
                    if q >= 2 and not last:
                        copy_xt(n, q - 2, q - 2)
                    for c in range(FCH):
                        ffn_gate(l, q, c)
                        if q == 3 and c == 0 and not last:
                            square(n, 0, 0, K0)
                            square(n, 0, 0, Q0)
                if not last:
                    nc.scalar.preload_act_table_set("natural_log_exp_and_others")
                    square(n, 0, 0, Q1)
                    guess_norm(n, 0, 0, 0)
                    square(n, 0, 0, K1)

            nc.scalar.preload_act_table_set("natural_log_exp_and_others")
            copy_xt(0, 0, 0)
            copy_xt(0, 1, 1)
            step(0, 0, 0)
            all_layers(act, layer)

        @block.gpsimd
        def _(pool):
            G = nc.gpsimd

            G.memset(ones[:], 1.0).then_inc(const_ready, 1)
            G.memset(minus_half[:], -0.5).then_inc(const_ready, 1)
            G.memset(three_halves[:], 1.5).then_inc(const_ready, 1)
            G.memset(half_shift[:], 0.5 * float(np.log(LN_SHIFT))).then_inc(const_ready, 1)

            def power(src, dst, steps, at):
                G.tensor_scalar(dst, src, EPS, None, ALU.add).then_inc(steps, 1)
                pool.wait_ge(steps, at)
                return G.tensor_tensor(dst, dst, minus_half[:], ALU.pow)

            pool.wait_ge(const_ready, 8)
            for n in range(2 * NQ):
                pool.wait_ge(c_var, n + 1)
                power(mv[:, n % 2, :, 1], rstd[:, n % 2, :], f_pow, n + 1).then_inc(c_rstd, 1)

            def ffn_power(l, q):
                wait_apart(pool, f_var, l * NQ + q + 1)
                power(mv[:, q % 2, :, 1], rstd[:, q % 2, :], f_pow, (l + 2) * NQ + q + 1).then_inc(f_rstd, 1)

            def split_weights(l, c):
                w = slice(CHUNK_COLS[c], CHUNK_COLS[c] + 512)
                G.tensor_copy(w_hi[:, w], wqkv[:, w]).then_inc(w_hi_ready, 1)
                pool.wait_ge(w_hi_ready, l * 6 + c + 1)
                G.tensor_tensor(w_lo[:, w], wqkv[:, w], w_hi[:, w], ALU.subtract).then_inc(w_ready, 1)

            def rotate(l, b, par, c):
                pool.wait_ge(rope_done[c], nth(l, b))
                G.tensor_tensor(t1[:, c, :], t1[:, c, :], t2[:, c, :], ALU.add).then_inc(qk_added[c], 1)

            def refine_norm(l, b, par, u):
                pool.wait_ge(rn_guess[u], nth(l, b))
                r = rn[:, par, u].rearrange("p a h -> p (a h)")
                s = ss[:, par, u].rearrange("p a h -> p (a h)")
                t = nt[:, u, :]
                G.tensor_tensor(t, r, r, ALU.mult).then_inc(newton[u], 1)
                pool.wait_ge(newton[u], nth(l, b, 3, -2))
                G.tensor_tensor(t, t, s, ALU.mult).then_inc(newton[u], 1)
                pool.wait_ge(newton[u], nth(l, b, 3, -1))
                G.tensor_tensor(t, t, three_halves[:], ALU.add).then_inc(newton[u], 1)
                pool.wait_ge(newton[u], nth(l, b, 3))
                G.tensor_tensor(r, r, t, ALU.mult).then_inc(rn_ready[u], 1)

            def normalise_k(l, b, par, u):
                c = 2 * u + 1
                pool.wait_ge(rn_ready[u], nth(l, b))
                pool.wait_ge(qk_added[c], nth(l, b))
                w = t1[:, c, :].rearrange("p (h e) -> p h e", h=8)
                G.tensor_tensor(w, w, rn[:, par, u, 1, :].unsqueeze(2).broadcast_to([P, 8, E]), ALU.mult).then_inc(k_ready[u], 1)

            def normalise_p(l, b, par, g):
                pool.wait_ge(rsum_ready[g], nth(l, b))
                w = pr[:, g]
                G.tensor_tensor(w, w, rsum[:, g, :].unsqueeze(2).broadcast_to([P, 4, P]), ALU.mult).then_inc(pr_ready[g], 1)

            def step(l, i, parity):
                run(l, i, parity, 1, rotate, Q1)
                run(l, i, parity, 1, normalise_k, 0)
                run(l, i, parity, 2, normalise_p, 0)
                run(l, i, parity, 2, normalise_p, 3)
                if last_step(i):
                    ffn_power(l, 0)
                run(l, i, parity, 1, refine_norm, 1)
                run(l, i, parity, 1, rotate, K1)
                run(l, i, parity, 1, normalise_k, 1)
                run(l, i, parity, 2, normalise_p, 2)
                if last_step(i):
                    ffn_power(l, 1)
                run(l, i, parity, 1, normalise_p, 1)
                run(l, i, parity, 0, rotate, Q0)
                run(l, i, parity, 0, rotate, K0)
                run(l, i, parity, 0, refine_norm, 0)

            def layer(l, last):
                n = l + 1
                steps(pool, l, step)
                if not last:
                    wait_apart(pool, ld_qkv, 16 * n + 16)
                    split_weights(n, 0)
                    split_weights(n, 1)
                ffn_power(l, 2)
                if not last:
                    split_weights(n, 2)
                    split_weights(n, 3)
                    split_weights(n, 4)
                ffn_power(l, 3)
                if not last:
                    split_weights(n, 5)
                    rotate(n, 0, 0, Q0)
                    rotate(n, 0, 0, K0)
                    refine_norm(n, 0, 0, 0)

            pool.wait_ge(ld_qkv, 16)
            for c in range(6):
                split_weights(0, c)
            step(0, 0, 0)
            all_layers(pool, layer)

        @block.vector
        def _(dve):
            V = nc.vector

            V.memset(zeros[:], 0.0).then_inc(zeroed, 1)
            dve.wait_ge(zeroed, 1)
            V.tensor_copy(xt_hi[E:P, :, 0:1], zeros[E:P, :].unsqueeze(2)).then_inc(const_ready, 1)
            V.tensor_copy(xt_lo[E:P, :, 0:1], zeros[E:P, :].unsqueeze(2)).then_inc(const_ready, 1)
            dve.wait_ge(ld_const, 80)
            V.tensor_copy(band16[:], consts[:, 0:P].unsqueeze(1).broadcast_to([P, 4, P])).then_inc(const_ready, 1)

            def stats(src, n):
                for b in range(QUAD):
                    V.bn_stats(st[:, n % 2, b, :], src(b)).then_inc(c_stats, 1)

            def aggregate(n, total, done):
                wait_apart(dve, c_stats, total)
                for b in range(QUAD):
                    i = V.bn_aggr(mv[:, n % 2, b, :], st[:, n % 2, b, :])
                i.then_inc(done, 1)

            def apply(dst, src, n):
                for b in range(QUAD):
                    i = V.tensor_scalar(dst(b), src(b), mv[:, n % 2, b, 0:1], rstd[:, n % 2, b:b + 1], ALU.subtract, ALU.mult)
                return i

            def cross_attention(q):
                s = slice(q * QUAD, (q + 1) * QUAD)
                dve.wait_ge(ld_x[q], 16)
                stats(lambda b: x1[:, q * QUAD + b, :], 2 * q)
                aggregate(2 * q, 4 * (2 * q + 1), c_var)
                dve.wait_ge(c_rstd, 2 * q + 1)
                apply(lambda b: xh[:, b, :], lambda b: x1[:, q * QUAD + b, :], 2 * q).then_inc(c_xn, 1)
                dve.wait_ge(c_s_ps, q + 1)
                V.tensor_reduce(nmax[:, 0, :], ps[:, 5, :].rearrange("p (b k) -> p b k", b=QUAD)[:, :, 0:CT], AX.X, ALU.max,
                                negate=True).then_inc(c_max, 1)
                dve.wait_ge(c_max, 2 * q + 1)
                V.tensor_scalar(nmax[:, 1, :], nmax[:, 0, :], float(P) ** -0.5, None, ALU.mult).then_inc(c_max, 1)
                dve.wait_ge(c_exp, 4 * q + 4)
                V.reciprocal(rsum[:, 0, :], psums[:, 0, :]).then_inc(c_sum, 1)
                dve.wait_ge(c_sum, q + 1)
                V.tensor_tensor(pr[:, 0, :, 0:CT], pr[:, 0, :, 0:CT], rsum[:, 0, :].unsqueeze(2).broadcast_to([P, QUAD, CT]),
                                ALU.mult).then_inc(c_pn, 1)
                dve.wait_ge(c_o_ps, q + 1)
                V.tensor_tensor(x1[:, s, :], x1[:, s, :], ps[:, 7, :].rearrange("p (b d) -> p b d", b=QUAD), ALU.add).then_inc(c_x1, 1)
                dve.wait_ge(c_x1, q + 1)
                stats(lambda b: x1[:, q * QUAD + b, :], 2 * q + 1)
                aggregate(2 * q + 1, 4 * (2 * q + 2), c_var)
                dve.wait_ge(c_rstd, 2 * q + 2)
                apply(lambda b: xr[:, q * QUAD + b, :], lambda b: x1[:, q * QUAD + b, :], 2 * q + 1).then_inc(x_final, 1)

            def rope_tables(l):
                dve.wait_ge(ld_scale, 16 * l + 16)
                for a in range(2):
                    V.tensor_tensor(rope[:, 2 * a, :], rope_base[:, 2 * a, :], qks[:, a, :], ALU.mult).then_inc(rope_ready, 1)
                    halves = lambda t: t.rearrange("p (a e) -> p a e", a=2)
                    V.tensor_tensor(halves(rope[:, 2 * a + 1, :]), halves(rope_base[:, 2 * a + 1, :]), halves(qks[:, a, :])[:, ::-1, :],
                                    ALU.mult).then_inc(rope_ready, 1)
                dve.wait_ge(rope_ready, 4 * l + 4)

            def copy_x(l, b, par):
                V.tensor_copy(xs[:, par, :], xr[:, b:b + 1, :] if isinstance(b, int) else xr[:, bass.ds(b, 1), :]).then_inc(xs_ready, 1)

            def lower_xt(l, b, par):
                dve.wait_ge(xt_hi_ready, nth(l, b))
                V.tensor_tensor(xt_lo[0:E, par, :], ps[0:E, X_BANK, 0:P], xt_hi[0:E, par, :], ALU.subtract)
                V.tensor_tensor(xt_lo[E:P, par, 1:P], ps[E:P, X_BANK, 0:P - 1], xt_hi[E:P, par, 1:P], ALU.subtract).then_inc(xt_ready, 1)

            def sum_squares(l, b, par, c):
                dve.wait_ge(sq_ready[c], nth(l, b))
                V.tensor_reduce(ss[:, par, c // 2, c % 2, :], sq[:, c, :].rearrange("p (h e) -> p h e", h=8), AX.X,
                                ALU.add).then_inc(ss_ready[c], 1)

            def clamp_norm(l, b, par, u):
                dve.wait_ge(ss_ready[2 * u], nth(l, b))
                dve.wait_ge(ss_ready[2 * u + 1], nth(l, b))
                w = ss[:, par, u].rearrange("p a h -> p (a h)")
                V.tensor_scalar(w, w, 1e-24, -0.5, ALU.max, ALU.mult).then_inc(ss_clamped[u], 1)

            def rotary(l, b, par, c):
                dve.wait_ge(sq_ready[c], nth(l, b))
                bank = ps[:, QKV_BANK[c], :]
                a = c % 2
                cos = rope[:, 2 * a, :].unsqueeze(1).broadcast_to([P, 8, E])
                V.tensor_tensor(t1[:, c, :].rearrange("p (h e) -> p h e", h=8), bank.rearrange("p (h e) -> p h e", h=8), cos, ALU.mult)
                sin = rope[:, 2 * a + 1, :].rearrange("p (a e) -> p a e", a=2).unsqueeze(1).broadcast_to([P, 8, 2, E // 2])
                V.tensor_tensor(t2[:, c, :].rearrange("p (h a e) -> p h a e", h=8, a=2),
                                bank.rearrange("p (h a e) -> p h a e", h=8, a=2)[:, :, ::-1, :], sin, ALU.mult).then_inc(rope_done[c], 1)

            def copy_v(l, b, par, s):
                dve.wait_ge(qkv_ps[V0 + s], nth(l, b))
                V.tensor_copy(v[:, par, s * 512:(s + 1) * 512], ps[:, QKV_BANK[V0 + s], :]).then_inc(v_ready[s], 1)

            def copy_qk(l, b, par, c):
                dve.wait_ge(tq_ps[c], nth(l, b))
                dst = (qT, kT)[c % 2]
                V.tensor_copy(dst[:, par, 4 * (c // 2):4 * (c // 2) + 4, :].rearrange("p a t -> p (a t)"),
                              ps[:, TQ_BANK[c], :]).then_inc(tq_ready[c], 1)

            def row_max(l, b, par, g):
                u = g // 2
                dve.wait_ge(s_ps[g], nth(l, b))
                V.tensor_reduce(nmax[:, g, :], ps[:, S_BANK[g], :].rearrange("p (h k) -> p h k", h=4), AX.X, ALU.max,
                                negate=True).then_inc(max_ready[g], 1)
                dve.wait_ge(rn_ready[u], nth(l, b))
                dve.wait_ge(max_ready[g], nth(l, b))
                V.tensor_tensor(nbias[:, g, :], nmax[:, g, :], rn[:, par, u, 0, g % 2::2], ALU.mult).then_inc(bias_ready[g], 1)

            def inverse_sum(l, b, par, g):
                dve.wait_ge(exp_ready[g], nth(l, b))
                V.reciprocal(rsum[:, g, :], psums[:, g, :]).then_inc(rsum_ready[g], 1)

            def copy_pT(l, b, par, g):
                dve.wait_ge(pt_ps[g], nth(l, b))
                V.tensor_copy(pT[:, g].rearrange("p a q -> p (a q)"), ps[:, TP_BANK[g], :]).then_inc(pt_ready[g], 1)

            def copy_o(l, b, par, s):
                dve.wait_ge(o_ps[s], nth(l, b))
                V.tensor_copy(oT[:, par, 4 * s:4 * s + 4, :].rearrange("p a t -> p (a t)"), ps[:, O_BANK[s], :]).then_inc(o_ready[s], 1)

            def add_residual(l, b, par):
                dve.wait_ge(y_ps, nth(l, b))
                w = xr[:, b:b + 1, :] if isinstance(b, int) else xr[:, bass.ds(b, 1), :]
                V.tensor_tensor(w, w, ps[:, Y_BANK, 0:P].unsqueeze(1), ALU.add).then_inc(x_updated, 1)

            def step(l, i, parity):
                if not x_ahead(i):
                    run(l, i, parity, 0, copy_x)
                run(l, i, parity, 1, sum_squares, K1)
                if not x_ahead(i):
                    run(l, i, parity, 0, lower_xt)
                run(l, i, parity, 1, clamp_norm, 1)
                run(l, i, parity, 1, copy_v, 0)
                run(l, i, parity, 2, row_max, 2)
                if last_step(i):
                    ffn_stats(l, 0)
                run(l, i, parity, 1, copy_qk, Q1)
                run(l, i, parity, 0, rotary, Q0)
                run(l, i, parity, 2, copy_pT, 0)
                run(l, i, parity, 2, inverse_sum, 2)
                if last_step(i):
                    ffn_normalise(l, 0)
                    ffn_stats(l, 1)
                run(l, i, parity, 1, row_max, 1)
                run(l, i, parity, 0, rotary, K0)
                run(l, i, parity, 0, sum_squares, Q1)
                run(l, i, parity, 0, sum_squares, K0)
                run(l, i, parity, 1, inverse_sum, 1)
                run(l, i, parity, 0, sum_squares, Q0)
                run(l, i, parity, 1, row_max, 0)
                run(l, i, parity, 0, clamp_norm, 0)
                if last_step(i):
                    ffn_affine(l, 0)
                run(l, i, parity, 2, copy_o, 1)
                run(l, i, parity, 0, rotary, Q1)
                run(l, i, parity, 1, inverse_sum, 0)
                run(l, i, parity, 1, row_max, 3)
                run(l, i, parity, 2, add_residual)
                run(l, i, parity, 0, rotary, K1)
                run(l, i, parity, 1, inverse_sum, 3)

            def ffn_stats(l, q):
                dve.wait_ge(f_shift_ps, l * NQ + q + 1)
                stats(lambda b: ps[:, q % 2, b * P:(b + 1) * P], q)
                aggregate(q, 8 * NQ + 4 * (l * NQ + q + 1), f_var)

            def ffn_normalise(l, q):
                dve.wait_ge(f_rstd, l * NQ + q + 1)
                if q >= 1:
                    dve.wait_ge(f_xhT_ps, l * NQ + q)
                apply(lambda b: xh[:, b, :], lambda b: ps[:, q % 2, b * P:(b + 1) * P], q).then_inc(f_xh, 1)

            def ffn_affine(l, q):
                if q == 0:
                    dve.wait_ge(ld_ffn, 64 * l + 64)
                dve.wait_ge(f_xhT_ps, l * NQ + q + 1)
                V.tensor_scalar(xhT[:, q % 2, :], ps[:, q % 2, :], vec[:, 0:1], vec[:, 1:2], ALU.mult, ALU.add).then_inc(f_xhT, 1)

            def ffn_gated(l, q, c):
                j = q * FCH + c
                dve.wait_ge(f_gate, (l * NQ + q) * FCH + c + 1)
                V.scalar_tensor_tensor(out=hT[:, q % 2, c, :], in0=ps[0:FC, 2 + j % 2, :], scalar=vec[0:FC, 2 + c:3 + c],
                                       in1=gate[:, j % 2, :], op0=ALU.add, op1=ALU.mult).then_inc(f_h, 1)

            def ffn_residual(l, q):
                dve.wait_ge(f_y_ps, l * NQ + q + 1)
                w = xr[:, q * QUAD:(q + 1) * QUAD, :]
                V.tensor_tensor(w, w, ps[:, 5, :].rearrange("p (b d) -> p b d", b=QUAD), ALU.add).then_inc(x_final, 1)

            dve.wait_ge(const_ready, 8)
            for q in range(NQ):
                cross_attention(q)
            def layer(l, last):
                n = l + 1
                steps(dve, l, step)
                for q in range(NQ + 1):
                    if q < NQ:
                        ffn_gated(l, q, 0)
                        if q + 1 < NQ:
                            ffn_normalise(l, q + 1)
                        elif not last:
                            rotary(n, 0, 0, K0)
                            sum_squares(n, 0, 0, K0)
                    if q >= 1:
                        ffn_residual(l, q - 1)
                        if q == 1 and not last:
                            dve.wait_ge(x_final, n * NQ + 1)
                            copy_x(n, 0, 0)
                            copy_x(n, 1, 1)
                        if last:
                            add_input(q - 1)
                    if q < NQ:
                        ffn_gated(l, q, 1)
                        if q + 1 < NQ:
                            ffn_affine(l, q + 1)
                        elif not last:
                            rotary(n, 0, 0, Q0)
                        ffn_gated(l, q, 2)
                        if q >= 2 and not last:
                            lower_xt(n, q - 2, q - 2)
                        if q + 2 < NQ:
                            ffn_stats(l, q + 2)
                        if q == 2 and not last:
                            rope_tables(n)
                        if q == 3 and not last:
                            sum_squares(n, 0, 0, Q0)
                            clamp_norm(n, 0, 0, 0)
                if not last:
                    rotary(n, 0, 0, Q1)
                    rotary(n, 0, 0, K1)
                    sum_squares(n, 0, 0, Q1)

            def add_input(q):
                s = slice(q * QUAD, (q + 1) * QUAD)
                dve.wait_ge(x_final, L * NQ + q + 1)
                V.tensor_tensor(x1[:, s, :], x1[:, s, :], xr[:, s, :], ALU.add).then_inc(final_sum, 1)

            rope_tables(0)
            copy_x(0, 0, 0)
            copy_x(0, 1, 1)
            lower_xt(0, 0, 0)
            lower_xt(0, 1, 1)
            step(0, 0, 0)
            all_layers(dve, layer)


def kernel(**inputs):
    import concourse.bacc as bacc
    from concourse.bass_utils import run_bass_kernel_spmd

    a = {k: np.ascontiguousarray(np.asarray(w)) for k, w in inputs.items()}
    w1 = np.zeros((L, P, 2, FCH * FC), np.float32)
    w1[:, :, :, :FI] = a["L0_ffn_W1"].reshape(L, P, 2, FI)
    b1 = np.zeros((L, 2, FCH * FC), np.float32)
    b1[:, :, :FI] = a["L0_ffn_b1"].reshape(L, 2, FI)
    w2 = np.zeros((L, FCH * FC, P), np.float32)
    w2[:, :FI] = a["L0_ffn_W2"]
    vec = np.zeros((L, P, 2 + 2 * FCH), np.float32)
    vec[:, :, 0] = a["L0_ffn_ln_g"]
    vec[:, :, 1] = a["L0_ffn_ln_b"]
    vec[:, :FC, 2:] = b1.reshape(L, 2 * FCH, FC).transpose(0, 2, 1)
    rope, const = constants()
    arrays = {
        "x_in": a["x"],
        "ctx_in": a["ctx_1024"],
        "xw_in": np.stack([a["L0_xattn_Wq"], a["L0_xattn_Wk"], a["L0_xattn_Wv"]], 1),
        "xv_in": np.stack([a["L0_xattn_bq"], a["L0_xattn_bk"]], 1),
        "bv_in": a["L0_xattn_bv"].reshape(1, P),
        "wqkv_in": a["L0_ffn_Wqkv"],
        "qk_scale_in": np.stack([a["L0_ffn_q_scale"], a["L0_ffn_k_scale"]], 1),
        "wo_in": a["L0_ffn_Wo"].reshape(L, 8, P, P).transpose(0, 2, 1, 3),
        "w1_in": w1.reshape(L, P, 2 * FCH, FC),
        "w2_in": w2.reshape(L, FCH, FC, P).transpose(0, 2, 1, 3),
        "vec_in": vec,
        "b2_in": a["L0_ffn_b2"].reshape(L, 1, P),
        "rope_in": rope,
        "const_in": const,
    }
    arrays = {k: np.ascontiguousarray(w) for k, w in arrays.items()}
    nc = bacc.Bacc("TRN2", target_bir_lowering=False, num_devices=1)
    args = [nc.dram_tensor(k, w.shape, F32, kind="ExternalInput").ap() for k, w in arrays.items()]
    out = nc.dram_tensor("out", (B, P, P), F32, kind="ExternalOutput").ap()
    build(nc, *args, out)
    r = run_bass_kernel_spmd(nc, [arrays], core_ids=[0])
    return r.results[0]["out"]
```

```python
import numpy as np
import concourse.bass as bass
from concourse import mybir
from concourse.alu_op_type import AluOpType as ALU

F32 = mybir.dt.float32
BF16 = mybir.dt.bfloat16
F32R = mybir.dt.float32r
ACT = mybir.ActivationFunctionType
AX = mybir.AxisListType

P = 128
B = 16
CT = 120
L = 6
H = 16
E = 64
WIN = 32
INNER = H * E
FI = 341
FCH = 3
FC = 114
QUAD = 4
NQ = B // QUAD
EPS = 1e-5
QK_SCALE = 8.0
MASKED = -1e25
LN_SHIFT = 2.0 ** 20

CHUNK_COLS = [0, INNER, 512, INNER + 512, 2 * INNER, 2 * INNER + 512]
Q0, K0, Q1, K1, V0, V1 = range(6)


def head(g, k):
    return 8 * (g // 2) + 2 * k + g % 2


def constants():
    half = np.arange(0, E, 2, dtype=np.float32)
    inv_freq = (np.float32(1.0) / np.power(np.float32(10000.0), half / np.float32(E))).astype(np.float32)
    t = np.arange(P, dtype=np.float32)
    fr = (t[:, None] * inv_freq[None, :]).astype(np.float32)
    fr = np.concatenate([fr, fr], -1)
    base = ((half + np.float32(0.4 * E)) / np.float32(1.4 * E)).astype(np.float32)
    power = ((t - P // 2) / np.float32(WIN // 2)).astype(np.float32)
    sc = np.power(base[None, :], power[:, None]).astype(np.float32)
    sc = np.concatenate([sc, sc], -1)
    cos, sin = np.cos(fr).astype(np.float32), np.sin(fr).astype(np.float32)
    sign = np.where(np.arange(E) < E // 2, -1.0, 1.0).astype(np.float32)
    inv = (np.float32(1.0) / sc).astype(np.float32)
    rope = np.stack([cos * sc * QK_SCALE, sin * sc * sign * QK_SCALE, cos * inv, sin * inv * sign], 1)
    q, k = np.arange(P)[:, None], np.arange(P)[None, :]
    band = np.where((k <= q) & (q <= k + WIN), 0.0, MASKED).astype(np.float32)
    ident = np.eye(P, dtype=np.float32)
    shift = np.eye(P, k=1, dtype=np.float32)
    return rope.astype(np.float32), np.concatenate([band, ident, shift], 1)


def build(nc, x_d, ctx_d, xw_d, xv_d, bv_d, wqkv_d, qk_scale_d, wo_d, w1_d, w2_d, vec_d, rope_d, const_d, out_d):
    def sb(name, shape, dt=F32):
        return nc.alloc_sbuf_tensor(name, shape, dt)

    x1 = sb("x1", [P, B, P])
    xr = sb("xr", [P, B, P])
    wqkv = sb("wqkv", [P, 3 * INNER])
    w_hi = sb("w_hi", [P, 3 * INNER], F32R)
    w_lo = sb("w_lo", [P, 3 * INNER], F32R)
    wo = sb("wo", [P, 8, P])
    w1 = sb("w1", [P, 2 * FCH, FC])
    w1_hi = sb("w1_hi", [P, 2 * FCH, FC], F32R)
    w1_lo = sb("w1_lo", [P, 2 * FCH, FC], F32R)
    w2 = sb("w2", [FC + 1, FCH, P])
    vec = sb("vec", [P, 2 + 2 * FCH])
    qks = sb("qks", [P, 2, E])
    rope_base = sb("rope_base", [P, 4, E])
    rope = sb("rope", [P, 4, E])
    consts = sb("consts", [P, 3 * P])
    ident = consts[:, P:2 * P]
    shift = consts[:, 2 * P:3 * P]
    ident16 = sb("ident16", [P, P], BF16)
    band16 = sb("band16", [P, 4, P], BF16)
    ones = sb("ones", [1, P])
    zeros = sb("zeros", [P, 2])
    half_shift = sb("half_shift", [P, 1])
    three_halves = sb("three_halves", [P, 16])
    minus_half = sb("minus_half", [P, QUAD])
    xs = sb("xs", [P, 2, P])
    xt_hi = sb("xt_hi", [P, 2, P], F32R)
    xt_lo = sb("xt_lo", [P, 2, P], F32R)
    sq = sb("sq", [P, 4, 512])
    ss = sb("ss", [P, 2, 2, 2, 8])
    rn = sb("rn", [P, 2, 2, 2, 8])
    nt = sb("nt", [P, 2, 16])
    t1 = sb("t1", [P, 4, 512])
    t2 = sb("t2", [P, 4, 512])
    qT = sb("qT", [P, 2, 8, P])
    kT = sb("kT", [P, 2, 8, P])
    v = sb("v", [P, 2, INNER])
    nmax = sb("nmax", [P, 4, 4])
    nbias = sb("nbias", [P, 4, 4])
    psums = sb("psums", [P, 4, 4])
    rsum = sb("rsum", [P, 4, 4])
    pr = sb("pr", [P, 4, 4, P])
    pT = sb("pT", [P, 4, 4, P])
    oT = sb("oT", [P, 2, 8, P])
    st = sb("st", [P, 2, QUAD, 6])
    mv = sb("mv", [P, 2, QUAD, 2])
    rstd = sb("rstd", [P, 2, QUAD])
    xh = sb("xh", [P, QUAD, P])
    xhT = sb("xhT", [P, 2, QUAD * P])
    xhT_hi = sb("xhT_hi", [P, 2, QUAD * P], F32R)
    xhT_lo = sb("xhT_lo", [P, 2, QUAD * P], F32R)
    gate = sb("gate", [FC, 2, QUAD * P])
    hT = sb("hT", [FC + 1, 2, FCH, QUAD * P])
    xw = sb("xw", [P, 3, P])
    xvec = sb("xvec", [P, 2])
    bv = sb("bv", [1, P])
    ctx = sb("ctx", [CT, 2, QUAD, P])
    ctxT = sb("ctxT", [P, QUAD * CT])
    xq = sb("xq", [P, 2, QUAD * P])
    xk = sb("xk", [P, 2, QUAD * CT])
    xvv = sb("xvv", [CT, 2, QUAD, P])

    ps = nc.alloc_psum_tensor("ps", [P, 8, 512], F32)
    X_BANK, Y_BANK = 6, 7
    QKV_BANK = [1, 0, 1, 0, 0, 1]
    TQ_BANK = [4, 4, 5, 4]
    S_BANK = [2, 3, 2, 3]
    TP_BANK = [4, 5, 5, 5]
    O_BANK = [7, 6]
    def sem(name):
        return nc.alloc_semaphore(name)

    ld_const, ld_qkv, ld_scale, ld_wo, ld_w1, ld_ffn = (
        sem(s) for s in ("ld_const", "ld_qkv", "ld_scale", "ld_wo", "ld_w1", "ld_ffn"))
    ld_x = [sem(f"ld_x{q}") for q in range(NQ)]
    ld_ctx = [sem(f"ld_ctx{q}") for q in range(2)]
    const_ready, x_final = sem("const_ready"), sem("x_final")
    rope_ready = sem("rope_ready")
    zeroed, exponent_ready, w_hi_ready, w_ready = sem("zeroed"), sem("exponent_ready"), sem("w_hi_ready"), sem("w_ready")

    def sems(name, n):
        return [sem(f"{name}{k}") for k in range(n)]

    xs_ready, xt_ps, xt_hi_ready, xt_ready = (sem(s) for s in ("xs_ready", "xt_ps", "xt_hi_ready", "xt_ready"))
    qkv_ps = sems("qkv_ps", 6)
    sq_ready, ss_ready, rope_done, qk_added, tq_ps, tq_ready = (
        sems(s, 4) for s in ("sq_ready", "ss_ready", "rope_done", "qk_added", "tq_ps", "tq_ready"))
    ss_clamped, ln_done, rn_guess, rn_ready, k_ready, v_ready = (
        sems(s, 2) for s in ("ss_clamped", "ln_done", "rn_guess", "rn_ready", "k_ready", "v_ready"))
    s_ps, max_ready, bias_ready, exp_ready, rsum_ready, pr_ready, pt_ps, pt_ready = (
        sems(s, 4) for s in ("s_ps", "max_ready", "bias_ready", "exp_ready", "rsum_ready", "pr_ready", "pt_ps", "pt_ready"))
    o_ps, o_ready = sems("o_ps", 2), sems("o_ready", 2)
    y_ps, x_updated = sem("y_ps"), sem("x_updated")
    newton = sems("newton", 2)
    f_shift_ps, f_stats, f_var, f_pow, f_rstd, f_xh, f_xhT_ps, f_xhT, f_h_ps, f_gate, f_h, f_y_ps = (
        sem("f_" + s) for s in ("shift_ps", "stats", "var", "pow", "rstd", "xh", "xhT_ps", "xhT", "h_ps", "gate", "h", "y_ps"))
    c_stats, c_var, c_rstd, c_xn, c_tr_ps, c_tr, c_qk_ps, c_qk, c_s_ps, c_max, c_exp, c_sum, c_pn, c_pT_ps, c_pT, c_o_ps, c_x1 = (
        sem("c_" + s) for s in ("stats", "var", "rstd", "xn", "tr_ps", "tr", "qk_ps", "qk", "s_ps", "max", "exp", "sum", "pn", "pT_ps", "pT", "o_ps", "x1"))
    f_hi, f_lo, w1_hi_ready, w1_ready = sem("f_hi"), sem("f_lo"), sem("w1_hi_ready"), sem("w1_ready")
    final_sum, stored, passed = sem("final_sum"), sem("stored"), sem("passed")

    def nth(l, b, per=1, k=0):
        return l * (B * per) + (b + 1) * per + k

    STEPS = B + 2
    HEAD_STEPS, TAIL_STEPS = 4, 2

    def live(i, lag):
        return not isinstance(i, int) or 0 <= i - lag < B

    def run(l, i, parity, lag, task, *args):
        if live(i, lag):
            task(l, i - lag, (parity + lag) % 2, *args)

    def bank_free(eng, l, i, *users):
        for semaphore, lag in users:
            if live(i, lag):
                eng.wait_ge(semaphore, nth(l, i - lag))
                return

    def x_ahead(i):
        return isinstance(i, int) and i <= 1

    def first_element(b):
        return isinstance(b, int) and b == 0

    def last_step(i):
        return isinstance(i, int) and i == STEPS - 1

    def steps(eng, l, step):
        for i in range(1, HEAD_STEPS):
            step(l, i, i % 2)
        with eng.Fori(0, (STEPS - HEAD_STEPS - TAIL_STEPS) // 2) as j:
            step(l, 2 * j + HEAD_STEPS, 0)
            step(l, 2 * j + (HEAD_STEPS + 1), 1)
        for i in range(STEPS - TAIL_STEPS, STEPS):
            step(l, i, i % 2)

    def all_layers(eng, layer):
        with eng.Fori(0, L - 1) as l:
            layer(l, False)
        layer(L - 1, True)

    def wait_apart(eng, semaphore, value):
        eng.wait_ge(semaphore, value)
        eng.sem_inc(passed, 1)

    block = nc.Block()
    with block as block:

        @block.sync
        def _(sp):
            sp.dma_start(x1[:, 0:QUAD, :], x_d[0:QUAD].rearrange("b t d -> t b d")).then_inc(ld_x[0], 16)
            sp.dma_start(consts[:], const_d).then_inc(ld_const, 16)
            sp.dma_start(xw[:], xw_d).then_inc(ld_const, 16)
            sp.dma_start(xvec[:], xv_d).then_inc(ld_const, 16)
            sp.dma_start(bv[:], bv_d).then_inc(ld_const, 16)
            sp.dma_start(rope_base[:], rope_d).then_inc(ld_const, 16)
            for q in range(NQ):
                if q >= 2:
                    sp.wait_ge(c_tr_ps, 2 * (q - 2) + 2)
                sp.dma_start(ctx[:, q % 2], ctx_d[q * QUAD:(q + 1) * QUAD].rearrange("b t d -> t b d")).then_inc(ld_ctx[q % 2], 16)
                if q + 1 < NQ:
                    s = slice((q + 1) * QUAD, (q + 2) * QUAD)
                    sp.dma_start(x1[:, s, :], x_d[s].rearrange("b t d -> t b d")).then_inc(ld_x[q + 1], 16)

            def load_rest(l):
                sp.dma_start(w2[:], w2_d[l]).then_inc(ld_ffn, 16)
                sp.dma_start(vec[:], vec_d[l]).then_inc(ld_ffn, 16)

            def load_scales(l):
                sp.dma_start(qks[:], qk_scale_d[l].unsqueeze(0).broadcast_to([P, 2, E])).then_inc(ld_scale, 16)

            sp.dma_start(wqkv[:], wqkv_d[0]).then_inc(ld_qkv, 16)
            load_scales(0)
            sp.dma_start(wo[:], wo_d[0]).then_inc(ld_wo, 16)
            sp.dma_start(w1[:], w1_d[0]).then_inc(ld_w1, 16)
            load_rest(0)
            with sp.Fori(1, L) as l:
                wait_apart(sp, w_ready, l * 6)
                sp.dma_start(wqkv[:], wqkv_d[l]).then_inc(ld_qkv, 16)
                wait_apart(sp, w1_ready, l)
                sp.dma_start(w1[:], w1_d[l]).then_inc(ld_w1, 16)
                wait_apart(sp, rope_ready, l * 4)
                load_scales(l)
                wait_apart(sp, y_ps, nth(l, -1))
                sp.dma_start(wo[:], wo_d[l]).then_inc(ld_wo, 16)
                wait_apart(sp, f_y_ps, l * NQ)
                wait_apart(sp, f_h, l * NQ * FCH)
                load_rest(l)
            for q in range(NQ):
                sp.wait_ge(final_sum, q + 1)
                s = slice(q * QUAD, (q + 1) * QUAD)
                sp.dma_start(out_d[s].rearrange("b t d -> t b d"), x1[:, s, :]).then_inc(stored, 16)
            sp.wait_ge(stored, 16 * NQ)

        @block.tensor
        def _(pe):
            mm, tr = nc.tensor.matmul, nc.tensor.transpose

            def cross_transpose(q):
                pe.wait_ge(c_xn, q + 1)
                for b in range(QUAD):
                    i = tr(ps[:, 0, b * P:(b + 1) * P], xh[:, b, :], ident)
                i.then_inc(c_tr_ps, 1)
                pe.wait_ge(ld_ctx[q % 2], 16 * (q // 2 + 1))
                for b in range(QUAD):
                    i = tr(ps[:, 1, b * CT:(b + 1) * CT], ctx[:, q % 2, b, :], ident[0:CT, 0:CT])
                i.then_inc(c_tr_ps, 1)

            def cross_project(q):
                pe.wait_ge(c_tr, 2 * q + 1)
                mm(ps[:, 2, :], xw[:, 0, :], xhT[:, 0, :], start=True, stop=True).then_inc(c_qk_ps, 1)
                pe.wait_ge(c_tr, 2 * q + 2)
                mm(ps[:, 3, 0:QUAD * CT], xw[:, 1, :], ctxT[:], start=True, stop=True).then_inc(c_qk_ps, 1)
                if q >= 1:
                    pe.wait_ge(c_qk, 3 * q)
                for b in range(QUAD):
                    o = ps[0:CT, 4, b * P:(b + 1) * P]
                    mm(o, ctxT[:, b * CT:(b + 1) * CT], xw[:, 2, :], start=True, stop=False)
                    i = mm(o, ones[0:1, 0:CT], bv[:], start=False, stop=True)
                i.then_inc(c_qk_ps, 1)

            def cross_scores(q):
                pe.wait_ge(c_qk, 3 * q + 2)
                for b in range(QUAD):
                    i = mm(ps[:, 5, b * P:b * P + CT], xq[:, q % 2, b * P:(b + 1) * P], xk[:, q % 2, b * CT:(b + 1) * CT],
                           start=True, stop=True)
                i.then_inc(c_s_ps, 1)

            def cross_weigh(q):
                pe.wait_ge(c_pn, q + 1)
                for b in range(QUAD):
                    i = tr(ps[0:CT, 6, b * P:(b + 1) * P], pr[:, 0, b, 0:CT], ident)
                i.then_inc(c_pT_ps, 1)
                pe.wait_ge(c_pT, q + 1)
                pe.wait_ge(c_qk, 3 * q + 3)
                if q >= 1:
                    pe.wait_ge(c_x1, q)
                for b in range(QUAD):
                    i = mm(ps[:, 7, b * P:(b + 1) * P], pT[0:CT, 0, b, :], xvv[:, q % 2, b, :], start=True, stop=True)
                i.then_inc(c_o_ps, 1)

            def transpose_x(l, b, par):
                pe.wait_ge(xs_ready, nth(l, b))
                tr(ps[:, X_BANK, 0:P], xs[:, par, :], ident).then_inc(xt_ps, 1)

            def project(l, b, par, c):
                if c == Q0 or first_element(b):
                    pe.wait_ge(xt_ready, nth(l, b))
                if first_element(b):
                    pe.wait_ge(w_ready, l * 6 + c + 1)
                w = slice(CHUNK_COLS[c], CHUNK_COLS[c] + 512)
                o = ps[:, QKV_BANK[c], :]
                mm(o, xt_hi[:, par, :], w_hi[:, w], start=True, stop=False)
                mm(o, xt_hi[:, par, :], w_lo[:, w], start=False, stop=False)
                mm(o, xt_lo[:, par, :], w_hi[:, w], start=False, stop=True).then_inc(qkv_ps[c], 1)

            def transpose_qk(l, b, par, c):
                pe.wait_ge(k_ready[c // 2] if c % 2 else qk_added[c], nth(l, b))
                for k in range(4):
                    i = tr(ps[:, TQ_BANK[c], k * P:(k + 1) * P], t1[:, c, k * P:(k + 1) * P], ident)
                i.then_inc(tq_ps[c], 1)

            def scores(l, b, par, g):
                u = g // 2
                pe.wait_ge(tq_ready[2 * u], nth(l, b))
                pe.wait_ge(tq_ready[2 * u + 1], nth(l, b))
                o = S_BANK[g]
                mm(ps[:, o, :], ident16[:], band16[:].rearrange("p a k -> p (a k)"), start=True, stop=False, skip_group_check=True)
                for k in range(4):
                    h = head(g, k)
                    r = slice(E * (h % 2), E * (h % 2) + E)
                    i = mm(ps[:, o, k * P:(k + 1) * P], qT[r, par, h // 2, :], kT[r, par, h // 2, :], start=False, stop=k == 3,
                           skip_group_check=True)
                i.then_inc(s_ps[g], 1)

            def transpose_p(l, b, par, g):
                pe.wait_ge(pr_ready[g], nth(l, b))
                for k in range(4):
                    i = tr(ps[:, TP_BANK[g], k * P:(k + 1) * P], pr[:, g, k, :], ident)
                i.then_inc(pt_ps[g], 1)

            def weigh_values(l, b, par, s):
                pe.wait_ge(pt_ready[2 * s], nth(l, b))
                pe.wait_ge(pt_ready[2 * s + 1], nth(l, b))
                pe.wait_ge(v_ready[s], nth(l, b))
                for k in range(4):
                    for odd in range(2):
                        g = 2 * s + odd
                        h = head(g, k)
                        i = mm(ps[odd * E:odd * E + E, O_BANK[s], k * P:(k + 1) * P], v[:, par, h * E:(h + 1) * E], pT[:, g, k, :],
                               start=True, stop=True)
                i.then_inc(o_ps[s], 1)

            def output_projection(l, b, par):
                pe.wait_ge(o_ready[0], nth(l, b))
                pe.wait_ge(o_ready[1], nth(l, b))
                for c in range(8):
                    i = mm(ps[:, Y_BANK, 0:P], oT[:, par, c, :], wo[:, c, :], start=c == 0, stop=c == 7)
                i.then_inc(y_ps, 1)

            def step(l, i, parity):
                if last_step(i):
                    ffn_shift(l, 0)
                if live(i, 1):
                    bank_free(pe, l, i, (tq_ready[K1], 2), (pt_ready[0], 3), (tq_ready[K0], 2), (tq_ready[Q0], 2))
                    transpose_qk(l, i - 1, 1 - parity, Q0)
                if live(i, 2):
                    bank_free(pe, l, i, (pt_ready[2], 3), (pt_ready[3], 3), (tq_ready[Q1], 2))
                    transpose_p(l, i - 2, parity, 1)
                if live(i, 2):
                    bank_free(pe, l, i, (exp_ready[0], 2))
                    scores(l, i - 2, parity, 2)
                if last_step(i):
                    ffn_shift(l, 1)
                if live(i, 0) and not x_ahead(i):
                    bank_free(pe, l, i, (o_ready[1], 3), (xt_ready, 1))
                    transpose_x(l, i, parity)
                if live(i, 1):
                    bank_free(pe, l, i, (rope_done[K1], 1))
                    project(l, i - 1, 1 - parity, V0)
                if live(i, 1):
                    bank_free(pe, l, i, (tq_ready[Q0], 1))
                    transpose_qk(l, i - 1, 1 - parity, K0)
                if live(i, 1):
                    bank_free(pe, l, i, (pt_ready[1], 2), (pt_ready[2], 3), (pt_ready[3], 3), (tq_ready[Q1], 2))
                    transpose_qk(l, i - 1, 1 - parity, Q1)
                if live(i, 0):
                    bank_free(pe, l, i, (v_ready[1], 2), (rope_done[Q1], 1), (rope_done[Q0], 1))
                    project(l, i, parity, Q0)
                if live(i, 0):
                    bank_free(pe, l, i, (v_ready[0], 1), (rope_done[K1], 1), (rope_done[K0], 1))
                    project(l, i, parity, K0)
                if live(i, 1):
                    bank_free(pe, l, i, (exp_ready[3], 2), (exp_ready[1], 2))
                    scores(l, i - 1, 1 - parity, 1)
                if live(i, 2):
                    bank_free(pe, l, i, (tq_ready[K0], 1), (tq_ready[Q0], 1), (tq_ready[K1], 2))
                    transpose_p(l, i - 2, parity, 0)
                if live(i, 2):
                    bank_free(pe, l, i, (tq_ready[Q1], 1), (pt_ready[1], 2))
                    transpose_p(l, i - 2, parity, 3)
                if live(i, 0):
                    bank_free(pe, l, i, (rope_done[Q0], 0))
                    project(l, i, parity, Q1)
                if live(i, 1):
                    bank_free(pe, l, i, (pt_ready[0], 2), (tq_ready[K0], 1))
                    transpose_qk(l, i - 1, 1 - parity, K1)
                if live(i, 2):
                    bank_free(pe, l, i, (x_updated, 3), (o_ready[0], 3))
                    weigh_values(l, i - 2, parity, 0)
                if last_step(i):
                    ffn_transpose(l, 0)
                if live(i, 2):
                    bank_free(pe, l, i, (pt_ready[3], 2))
                    transpose_p(l, i - 2, parity, 2)
                if live(i, 0):
                    bank_free(pe, l, i, (rope_done[K0], 0))
                    project(l, i, parity, K1)
                if live(i, 1):
                    bank_free(pe, l, i, (exp_ready[2], 2), (exp_ready[0], 2))
                    scores(l, i - 1, 1 - parity, 0)
                if live(i, 2):
                    bank_free(pe, l, i, (xt_ready, 0), (o_ready[1], 3))
                    weigh_values(l, i - 2, parity, 1)
                if last_step(i):
                    ffn_up(l, 0, 0)
                if live(i, 1):
                    bank_free(pe, l, i, (exp_ready[1], 1))
                    scores(l, i - 1, 1 - parity, 3)
                if live(i, 2):
                    bank_free(pe, l, i, (o_ready[0], 2))
                    output_projection(l, i - 2, parity)
                if live(i, 1):
                    bank_free(pe, l, i, (rope_done[Q1], 0), (rope_done[Q0], 0), (v_ready[1], 2))
                    project(l, i - 1, 1 - parity, V1)

            def ffn_shift(l, q):
                pe.wait_ge(x_updated, nth(l, QUAD * q + QUAD - 1))
                if q >= 2:
                    pe.wait_ge(f_xhT, l * NQ + q - 1)
                else:
                    pe.wait_ge(v_ready[q], nth(l, B - 1))
                s = slice(q * QUAD, (q + 1) * QUAD)
                o = ps[:, q % 2, :].rearrange("p (b d) -> p b d", b=QUAD)
                mm(o[:, :, 0:E], ident, xr[:, s, 0:E], start=True, stop=True)
                mm(o[:, :, E:P], shift, xr[:, s, E:P], start=True, stop=True).then_inc(f_shift_ps, 1)

            def ffn_transpose(l, q):
                pe.wait_ge(f_xh, l * NQ + q + 1)
                for b in range(QUAD):
                    i = tr(ps[:, q % 2, b * P:(b + 1) * P], xh[:, b, :], ident)
                i.then_inc(f_xhT_ps, 1)

            def ffn_up(l, q, c):
                j = q * FCH + c
                if c == 0:
                    if q == 0:
                        pe.wait_ge(w1_ready, l + 1)
                        pe.wait_ge(ld_ffn, 32 * l + 32)
                    pe.wait_ge(f_lo, l * NQ + q + 1)
                if j == 1:
                    pe.wait_ge(x_updated, nth(l, B - 1))
                if j >= 2:
                    pe.wait_ge(f_h, (l * NQ + q) * FCH + c - 1)
                for o, cc in ((ps[0:FC, [4, 7][j % 2], :], FCH + c), (ps[0:FC, 2 + j % 2, :], c)):
                    mm(o, w1_hi[:, cc, :], xhT_hi[:, q % 2, :], start=True, stop=False)
                    mm(o, w1_lo[:, cc, :], xhT_hi[:, q % 2, :], start=False, stop=False)
                    i = mm(o, w1_hi[:, cc, :], xhT_lo[:, q % 2, :], start=False, stop=True)
                i.then_inc(f_h_ps, 1)

            def ffn_down(l, q):
                pe.wait_ge(f_h, (l * NQ + q + 1) * FCH)
                if q >= 1:
                    pe.wait_ge(x_final, (l + 1) * NQ + q)
                for b in range(QUAD):
                    o = ps[:, 5, b * P:(b + 1) * P]
                    for c in range(FCH):
                        k = FC + 1 if c == 0 else FC
                        i = mm(o, hT[0:k, q % 2, c, b * P:(b + 1) * P], w2[0:k, c, :], start=c == 0, stop=c == FCH - 1)
                i.then_inc(f_y_ps, 1)

            pe.wait_ge(ld_const, 80)
            pe.wait_ge(const_ready, 8)
            cross_transpose(0)
            cross_project(0)
            for q in range(NQ):
                if q + 1 < NQ:
                    cross_transpose(q + 1)
                cross_scores(q)
                if q + 1 < NQ:
                    cross_project(q + 1)
                cross_weigh(q)

            def layer(l, last):
                n = l + 1
                pe.wait_ge(x_final, n * NQ)
                pe.wait_ge(ld_wo, 16 * n)
                steps(pe, l, step)
                for q in range(NQ + 1):
                    if q == 2 and not last:
                        transpose_x(n, 0, 0)
                    if q == 3 and not last:
                        project(n, 0, 0, K0)
                    if 1 <= q < NQ:
                        ffn_up(l, q, 0)
                    if q == 3 and not last:
                        transpose_x(n, 1, 1)
                        project(n, 0, 0, Q0)
                    if q == NQ and not last:
                        pe.wait_ge(rope_done[Q0], nth(n, 0))
                        project(n, 0, 0, Q1)
                        pe.wait_ge(rope_done[K0], nth(n, 0))
                        project(n, 0, 0, K1)
                    if q >= 1:
                        ffn_down(l, q - 1)
                    if q + 1 < NQ:
                        ffn_transpose(l, q + 1)
                    if q < NQ:
                        ffn_up(l, q, 1)
                    if q + 2 < NQ:
                        ffn_shift(l, q + 2)
                    if q < NQ:
                        ffn_up(l, q, 2)

            pe.wait_ge(x_final, NQ)
            transpose_x(0, 0, 0)
            pe.wait_ge(xt_ready, 1)
            transpose_x(0, 1, 1)
            step(0, 0, 0)
            all_layers(pe, layer)

        @block.scalar
        def _(act):
            A = nc.scalar.activation

            def cross_copy_inputs(q):
                act.wait_ge(c_tr_ps, 2 * q + 1)
                A(xhT[:, 0, :], ps[:, 0, :], ACT.Copy).then_inc(c_tr, 1)
                act.wait_ge(c_tr_ps, 2 * q + 2)
                A(ctxT[:], ps[:, 1, 0:QUAD * CT], ACT.Copy).then_inc(c_tr, 1)

            def cross_copy_qkv(q):
                act.wait_ge(c_qk_ps, 3 * q + 1)
                A(xq[:, q % 2], ps[:, 2, :], ACT.Identity, bias=xvec[:, 0:1]).then_inc(c_qk, 1)
                act.wait_ge(c_qk_ps, 3 * q + 2)
                A(xk[:, q % 2], ps[:, 3, 0:QUAD * CT], ACT.Identity, bias=xvec[:, 1:2]).then_inc(c_qk, 1)
                act.wait_ge(c_qk_ps, 3 * q + 3)
                A(xvv[:, q % 2].rearrange("p b d -> p (b d)"), ps[0:CT, 4, :], ACT.Copy).then_inc(c_qk, 1)

            def cross_exps(q):
                act.wait_ge(c_max, 2 * q + 2)
                for b in range(QUAD):
                    A(pr[:, 0, b, 0:CT], ps[:, 5, b * P:b * P + CT], ACT.Exp, bias=nmax[:, 1, b:b + 1],
                      scale=float(P) ** -0.5, accum_out=psums[:, 0, b:b + 1]).then_inc(c_exp, 1)

            def cross_copy_pT(q):
                act.wait_ge(c_pT_ps, q + 1)
                A(pT[0:CT, 0].rearrange("p b d -> p (b d)"), ps[0:CT, 6, :], ACT.Copy).then_inc(c_pT, 1)

            def copy_xt(l, b, par):
                act.wait_ge(xt_ps, nth(l, b))
                A(xt_hi[0:E, par, :], ps[0:E, X_BANK, 0:P], ACT.Copy)
                A(xt_hi[E:P, par, 1:P], ps[E:P, X_BANK, 0:P - 1], ACT.Copy).then_inc(xt_hi_ready, 1)

            def square(l, b, par, c):
                act.wait_ge(qkv_ps[c], nth(l, b))
                A(sq[:, c, :], ps[:, QKV_BANK[c], :], ACT.Square).then_inc(sq_ready[c], 1)

            def guess_norm(l, b, par, u):
                act.wait_ge(ss_clamped[u], nth(l, b))
                r = rn[:, par, u].rearrange("p a h -> p (a h)")
                A(r, ss[:, par, u].rearrange("p a h -> p (a h)"), ACT.Ln, scale=-2.0 * LN_SHIFT).then_inc(ln_done[u], 1)
                act.wait_ge(ln_done[u], nth(l, b))
                A(r, r, ACT.Exp, scale=-0.5, bias=half_shift[:, 0:1]).then_inc(rn_guess[u], 1)

            def copy_v(l, b, par, s):
                act.wait_ge(qkv_ps[V0 + s], nth(l, b))
                A(v[:, par, s * 512:(s + 1) * 512], ps[:, QKV_BANK[V0 + s], :], ACT.Copy).then_inc(v_ready[s], 1)

            def copy_qk(l, b, par, c):
                act.wait_ge(tq_ps[c], nth(l, b))
                dst = (qT, kT)[c % 2]
                A(dst[:, par, 4 * (c // 2):4 * (c // 2) + 4, :].rearrange("p a t -> p (a t)"), ps[:, TQ_BANK[c], :],
                  ACT.Copy).then_inc(tq_ready[c], 1)

            def exps(l, b, par, g):
                act.wait_ge(bias_ready[g], nth(l, b))
                for k in range(4):
                    i = A(pr[:, g, k, :], ps[:, S_BANK[g], k * P:(k + 1) * P], ACT.Exp, bias=nbias[:, g, k:k + 1],
                          scale=rn[:, par, g // 2, 0, 2 * k + g % 2:2 * k + g % 2 + 1], accum_out=psums[:, g, k:k + 1])
                i.then_inc(exp_ready[g], 1)

            def copy_pT(l, b, par, g):
                act.wait_ge(pt_ps[g], nth(l, b))
                A(pT[:, g].rearrange("p a q -> p (a q)"), ps[:, TP_BANK[g], :], ACT.Copy).then_inc(pt_ready[g], 1)

            def copy_o(l, b, par, s):
                act.wait_ge(o_ps[s], nth(l, b))
                A(oT[:, par, 4 * s:4 * s + 4, :].rearrange("p a t -> p (a t)"), ps[:, O_BANK[s], :], ACT.Copy).then_inc(o_ready[s], 1)

            def step(l, i, parity):
                run(l, i, parity, 1, copy_qk, Q0)
                run(l, i, parity, 2, copy_pT, 1)
                if not x_ahead(i):
                    run(l, i, parity, 0, copy_xt)
                run(l, i, parity, 2, copy_v, 1)
                run(l, i, parity, 1, guess_norm, 1)
                run(l, i, parity, 1, copy_qk, K0)
                run(l, i, parity, 0, square, Q0)
                run(l, i, parity, 2, exps, 2)
                if last_step(i):
                    nc.scalar.preload_act_table(ACT.Gelu)
                run(l, i, parity, 0, square, K0)
                run(l, i, parity, 2, copy_pT, 3)
                run(l, i, parity, 0, square, Q1)
                run(l, i, parity, 1, exps, 1)
                run(l, i, parity, 1, copy_qk, K1)
                run(l, i, parity, 2, copy_pT, 2)
                if last_step(i):
                    ffn_upper(l, 0)
                run(l, i, parity, 2, copy_o, 0)
                run(l, i, parity, 1, exps, 0)
                run(l, i, parity, 0, guess_norm, 0)
                run(l, i, parity, 0, square, K1)
                run(l, i, parity, 1, exps, 3)

            def ffn_upper(l, q):
                act.wait_ge(f_xhT, l * NQ + q + 1)
                A(xhT_hi[:, q % 2, :], xhT[:, q % 2, :], ACT.Copy).then_inc(f_hi, 1)

            def ffn_gate(l, q, c):
                j = q * FCH + c
                act.wait_ge(f_h_ps, (l * NQ + q) * FCH + c + 1)
                if j >= 2:
                    act.wait_ge(f_h, (l * NQ + q) * FCH + c - 1)
                A(gate[:, j % 2, :], ps[0:FC, [4, 7][j % 2], :], ACT.Gelu, bias=vec[0:FC, 2 + FCH + c:3 + FCH + c]).then_inc(f_gate, 1)

            act.wait_ge(ld_const, 80)
            A(ident16[:], ident, ACT.Copy).then_inc(const_ready, 1)
            act.wait_ge(const_ready, 8)
            cross_copy_inputs(0)
            cross_copy_qkv(0)
            for q in range(NQ):
                if q + 1 < NQ:
                    cross_copy_inputs(q + 1)
                cross_exps(q)
                if q + 1 < NQ:
                    cross_copy_qkv(q + 1)
                cross_copy_pT(q)

            def layer(l, last):
                n = l + 1
                steps(act, l, step)
                act.wait_ge(ld_ffn, 32 * n)
                for q in range(NQ):
                    if q == 2 and not last:
                        copy_xt(n, 0, 0)
                    for c in range(FCH):
                        ffn_gate(l, q, c)
                        if c == 0 and q + 1 < NQ:
                            ffn_upper(l, q + 1)
                        if q == 3 and c == 0 and not last:
                            square(n, 0, 0, K0)
                            copy_xt(n, 1, 1)
                            square(n, 0, 0, Q0)
                if not last:
                    nc.scalar.preload_act_table_set("natural_log_exp_and_others")
                    square(n, 0, 0, Q1)
                    guess_norm(n, 0, 0, 0)
                    square(n, 0, 0, K1)

            nc.scalar.preload_act_table_set("natural_log_exp_and_others")
            copy_xt(0, 0, 0)
            copy_xt(0, 1, 1)
            step(0, 0, 0)
            all_layers(act, layer)

        @block.gpsimd
        def _(pool):
            G = nc.gpsimd

            G.memset(ones[:], 1.0).then_inc(const_ready, 1)
            G.memset(minus_half[:], -0.5).then_inc(exponent_ready, 1)
            G.memset(three_halves[:], 1.5).then_inc(const_ready, 1)
            G.memset(half_shift[:], 0.5 * float(np.log(LN_SHIFT))).then_inc(const_ready, 1)

            def power(src, dst, steps, at):
                G.tensor_scalar(dst, src, EPS, None, ALU.add).then_inc(steps, 1)
                pool.wait_ge(steps, at)
                return G.tensor_tensor(dst, dst, minus_half[:], ALU.pow)

            def ffn_power(l, q):
                wait_apart(pool, f_var, l * NQ + q + 1)
                power(mv[:, q % 2, :, 1], rstd[:, q % 2, :], f_pow, (l + 2) * NQ + q + 1).then_inc(f_rstd, 1)

            def upper_w1(l):
                wait_apart(pool, ld_w1, 16 * l + 16)
                G.tensor_copy(w1_hi[:], w1[:]).then_inc(w1_hi_ready, 1)

            def lower_w1(l):
                pool.wait_ge(w1_hi_ready, l + 1)
                G.tensor_tensor(w1_lo[:], w1[:], w1_hi[:], ALU.subtract).then_inc(w1_ready, 1)

            def split_weights(l, c):
                w = slice(CHUNK_COLS[c], CHUNK_COLS[c] + 512)
                G.tensor_copy(w_hi[:, w], wqkv[:, w]).then_inc(w_hi_ready, 1)
                pool.wait_ge(w_hi_ready, l * 6 + c + 1)
                G.tensor_tensor(w_lo[:, w], wqkv[:, w], w_hi[:, w], ALU.subtract).then_inc(w_ready, 1)

            def rotate(l, b, par, c):
                pool.wait_ge(rope_done[c], nth(l, b))
                G.tensor_tensor(t1[:, c, :], t1[:, c, :], t2[:, c, :], ALU.add).then_inc(qk_added[c], 1)

            def refine_norm(l, b, par, u):
                pool.wait_ge(rn_guess[u], nth(l, b))
                r = rn[:, par, u].rearrange("p a h -> p (a h)")
                s = ss[:, par, u].rearrange("p a h -> p (a h)")
                t = nt[:, u, :]
                G.tensor_tensor(t, r, r, ALU.mult).then_inc(newton[u], 1)
                pool.wait_ge(newton[u], nth(l, b, 3, -2))
                G.tensor_tensor(t, t, s, ALU.mult).then_inc(newton[u], 1)
                pool.wait_ge(newton[u], nth(l, b, 3, -1))
                G.tensor_tensor(t, t, three_halves[:], ALU.add).then_inc(newton[u], 1)
                pool.wait_ge(newton[u], nth(l, b, 3))
                G.tensor_tensor(r, r, t, ALU.mult).then_inc(rn_ready[u], 1)

            def normalise_k(l, b, par, u):
                c = 2 * u + 1
                pool.wait_ge(rn_ready[u], nth(l, b))
                pool.wait_ge(qk_added[c], nth(l, b))
                w = t1[:, c, :].rearrange("p (h e) -> p h e", h=8)
                G.tensor_tensor(w, w, rn[:, par, u, 1, :].unsqueeze(2).broadcast_to([P, 8, E]), ALU.mult).then_inc(k_ready[u], 1)

            def normalise_p(l, b, par, g):
                pool.wait_ge(rsum_ready[g], nth(l, b))
                w = pr[:, g]
                G.tensor_tensor(w, w, rsum[:, g, :].unsqueeze(2).broadcast_to([P, 4, P]), ALU.mult).then_inc(pr_ready[g], 1)

            def step(l, i, parity):
                run(l, i, parity, 1, rotate, Q1)
                run(l, i, parity, 1, normalise_k, 0)
                run(l, i, parity, 2, normalise_p, 0)
                run(l, i, parity, 2, normalise_p, 3)
                if last_step(i):
                    ffn_power(l, 0)
                run(l, i, parity, 1, refine_norm, 1)
                run(l, i, parity, 1, rotate, K1)
                run(l, i, parity, 1, normalise_k, 1)
                run(l, i, parity, 2, normalise_p, 2)
                if isinstance(i, int) and i == 2:
                    upper_w1(l)
                if isinstance(i, int) and i == 3:
                    lower_w1(l)
                if last_step(i):
                    ffn_power(l, 1)
                run(l, i, parity, 1, normalise_p, 1)
                run(l, i, parity, 0, rotate, Q0)
                run(l, i, parity, 0, rotate, K0)
                run(l, i, parity, 0, refine_norm, 0)

            def layer(l, last):
                n = l + 1
                steps(pool, l, step)
                if not last:
                    wait_apart(pool, ld_qkv, 16 * n + 16)
                    split_weights(n, 0)
                    split_weights(n, 1)
                    split_weights(n, 2)
                ffn_power(l, 2)
                if not last:
                    split_weights(n, 3)
                    split_weights(n, 4)
                ffn_power(l, 3)
                if not last:
                    split_weights(n, 5)
                    rotate(n, 0, 0, K0)
                    rotate(n, 0, 0, Q0)
                    refine_norm(n, 0, 0, 0)

            pool.wait_ge(exponent_ready, 1)
            for n in range(2 * NQ):
                pool.wait_ge(c_var, n + 1)
                power(mv[:, n % 2, :, 1], rstd[:, n % 2, :], f_pow, n + 1).then_inc(c_rstd, 1)
                if n in (3, 5, 6):
                    if n == 3:
                        pool.wait_ge(ld_qkv, 16)
                    c = {3: 0, 5: 2, 6: 4}[n]
                    split_weights(0, c)
                    split_weights(0, c + 1)
            pool.wait_ge(const_ready, 8)
            step(0, 0, 0)
            all_layers(pool, layer)

        @block.vector
        def _(dve):
            V = nc.vector

            V.memset(zeros[:], 0.0).then_inc(zeroed, 1)
            V.memset(hT[96:FC + 1, :, 0, :], 1.0).then_inc(const_ready, 1)
            dve.wait_ge(zeroed, 1)
            V.tensor_copy(xt_hi[E:P, :, 0:1], zeros[E:P, :].unsqueeze(2)).then_inc(const_ready, 1)
            V.tensor_copy(xt_lo[E:P, :, 0:1], zeros[E:P, :].unsqueeze(2)).then_inc(const_ready, 1)
            def stats(src, n):
                for b in range(QUAD):
                    V.bn_stats(st[:, n % 2, b, :], src(b)).then_inc(c_stats, 1)

            def aggregate(n, total, done):
                wait_apart(dve, c_stats, total)
                for b in range(QUAD):
                    i = V.bn_aggr(mv[:, n % 2, b, :], st[:, n % 2, b, :])
                i.then_inc(done, 1)

            def apply(dst, src, n):
                for b in range(QUAD):
                    i = V.tensor_scalar(dst(b), src(b), mv[:, n % 2, b, 0:1], rstd[:, n % 2, b:b + 1], ALU.subtract, ALU.mult)
                return i

            NORM_X, NORM_OUT = [0, 1, 2, 4], [3, 5, 6, 7]

            def cross_stats_x(q):
                dve.wait_ge(ld_x[q], 16)
                n = NORM_X[q]
                stats(lambda b: x1[:, q * QUAD + b, :], n)
                aggregate(n, 4 * (n + 1), c_var)

            def cross_normalise_x(q):
                n = NORM_X[q]
                dve.wait_ge(c_rstd, n + 1)
                if q >= 1:
                    dve.wait_ge(c_tr_ps, 2 * q - 1)
                apply(lambda b: xh[:, b, :], lambda b: x1[:, q * QUAD + b, :], n).then_inc(c_xn, 1)

            def cross_max(q):
                dve.wait_ge(c_s_ps, q + 1)
                V.tensor_reduce(nmax[:, 0, :], ps[:, 5, :].rearrange("p (b k) -> p b k", b=QUAD)[:, :, 0:CT], AX.X, ALU.max,
                                negate=True).then_inc(c_max, 1)
                dve.wait_ge(c_max, 2 * q + 1)
                V.tensor_scalar(nmax[:, 1, :], nmax[:, 0, :], float(P) ** -0.5, None, ALU.mult).then_inc(c_max, 1)

            def cross_normalise_p(q):
                dve.wait_ge(c_exp, 4 * q + 4)
                V.reciprocal(rsum[:, 0, :], psums[:, 0, :]).then_inc(c_sum, 1)
                dve.wait_ge(c_sum, q + 1)
                V.tensor_tensor(pr[:, 0, :, 0:CT], pr[:, 0, :, 0:CT], rsum[:, 0, :].unsqueeze(2).broadcast_to([P, QUAD, CT]),
                                ALU.mult).then_inc(c_pn, 1)

            def cross_add(q):
                s = slice(q * QUAD, (q + 1) * QUAD)
                n = NORM_OUT[q]
                dve.wait_ge(c_o_ps, q + 1)
                V.tensor_tensor(x1[:, s, :], x1[:, s, :], ps[:, 7, :].rearrange("p (b d) -> p b d", b=QUAD), ALU.add).then_inc(c_x1, 1)
                dve.wait_ge(c_x1, q + 1)
                stats(lambda b: x1[:, q * QUAD + b, :], n)
                aggregate(n, 4 * (n + 1), c_var)

            def cross_normalise_out(q):
                n = NORM_OUT[q]
                dve.wait_ge(c_rstd, n + 1)
                apply(lambda b: xr[:, q * QUAD + b, :], lambda b: x1[:, q * QUAD + b, :], n).then_inc(x_final, 1)

            def rope_tables(l):
                dve.wait_ge(ld_scale, 16 * l + 16)
                for a in range(2):
                    V.tensor_tensor(rope[:, 2 * a, :], rope_base[:, 2 * a, :], qks[:, a, :], ALU.mult).then_inc(rope_ready, 1)
                    halves = lambda t: t.rearrange("p (a e) -> p a e", a=2)
                    V.tensor_tensor(halves(rope[:, 2 * a + 1, :]), halves(rope_base[:, 2 * a + 1, :]), halves(qks[:, a, :])[:, ::-1, :],
                                    ALU.mult).then_inc(rope_ready, 1)
                dve.wait_ge(rope_ready, 4 * l + 4)

            def copy_x(l, b, par):
                V.tensor_copy(xs[:, par, :], xr[:, b:b + 1, :] if isinstance(b, int) else xr[:, bass.ds(b, 1), :]).then_inc(xs_ready, 1)

            def lower_xt(l, b, par):
                dve.wait_ge(xt_hi_ready, nth(l, b))
                V.tensor_tensor(xt_lo[0:E, par, :], ps[0:E, X_BANK, 0:P], xt_hi[0:E, par, :], ALU.subtract)
                V.tensor_tensor(xt_lo[E:P, par, 1:P], ps[E:P, X_BANK, 0:P - 1], xt_hi[E:P, par, 1:P], ALU.subtract).then_inc(xt_ready, 1)

            def sum_squares(l, b, par, c):
                dve.wait_ge(sq_ready[c], nth(l, b))
                V.tensor_reduce(ss[:, par, c // 2, c % 2, :], sq[:, c, :].rearrange("p (h e) -> p h e", h=8), AX.X,
                                ALU.add).then_inc(ss_ready[c], 1)

            def clamp_norm(l, b, par, u):
                dve.wait_ge(ss_ready[2 * u], nth(l, b))
                dve.wait_ge(ss_ready[2 * u + 1], nth(l, b))
                w = ss[:, par, u].rearrange("p a h -> p (a h)")
                V.tensor_scalar(w, w, 1e-24, -0.5, ALU.max, ALU.mult).then_inc(ss_clamped[u], 1)

            def rotary(l, b, par, c):
                dve.wait_ge(sq_ready[c], nth(l, b))
                bank = ps[:, QKV_BANK[c], :]
                a = c % 2
                cos = rope[:, 2 * a, :].unsqueeze(1).broadcast_to([P, 8, E])
                V.tensor_tensor(t1[:, c, :].rearrange("p (h e) -> p h e", h=8), bank.rearrange("p (h e) -> p h e", h=8), cos, ALU.mult)
                sin = rope[:, 2 * a + 1, :].rearrange("p (a e) -> p a e", a=2).unsqueeze(1).broadcast_to([P, 8, 2, E // 2])
                V.tensor_tensor(t2[:, c, :].rearrange("p (h a e) -> p h a e", h=8, a=2),
                                bank.rearrange("p (h a e) -> p h a e", h=8, a=2)[:, :, ::-1, :], sin, ALU.mult).then_inc(rope_done[c], 1)

            def copy_v(l, b, par, s):
                dve.wait_ge(qkv_ps[V0 + s], nth(l, b))
                V.tensor_copy(v[:, par, s * 512:(s + 1) * 512], ps[:, QKV_BANK[V0 + s], :]).then_inc(v_ready[s], 1)

            def copy_qk(l, b, par, c):
                dve.wait_ge(tq_ps[c], nth(l, b))
                dst = (qT, kT)[c % 2]
                V.tensor_copy(dst[:, par, 4 * (c // 2):4 * (c // 2) + 4, :].rearrange("p a t -> p (a t)"),
                              ps[:, TQ_BANK[c], :]).then_inc(tq_ready[c], 1)

            def row_max(l, b, par, g):
                u = g // 2
                dve.wait_ge(s_ps[g], nth(l, b))
                V.tensor_reduce(nmax[:, g, :], ps[:, S_BANK[g], :].rearrange("p (h k) -> p h k", h=4), AX.X, ALU.max,
                                negate=True).then_inc(max_ready[g], 1)
                dve.wait_ge(rn_ready[u], nth(l, b))
                dve.wait_ge(max_ready[g], nth(l, b))
                V.tensor_tensor(nbias[:, g, :], nmax[:, g, :], rn[:, par, u, 0, g % 2::2], ALU.mult).then_inc(bias_ready[g], 1)

            def inverse_sum(l, b, par, g):
                dve.wait_ge(exp_ready[g], nth(l, b))
                V.reciprocal(rsum[:, g, :], psums[:, g, :]).then_inc(rsum_ready[g], 1)

            def copy_pT(l, b, par, g):
                dve.wait_ge(pt_ps[g], nth(l, b))
                V.tensor_copy(pT[:, g].rearrange("p a q -> p (a q)"), ps[:, TP_BANK[g], :]).then_inc(pt_ready[g], 1)

            def copy_o(l, b, par, s):
                dve.wait_ge(o_ps[s], nth(l, b))
                V.tensor_copy(oT[:, par, 4 * s:4 * s + 4, :].rearrange("p a t -> p (a t)"), ps[:, O_BANK[s], :]).then_inc(o_ready[s], 1)

            def add_residual(l, b, par):
                dve.wait_ge(y_ps, nth(l, b))
                w = xr[:, b:b + 1, :] if isinstance(b, int) else xr[:, bass.ds(b, 1), :]
                V.tensor_tensor(w, w, ps[:, Y_BANK, 0:P].unsqueeze(1), ALU.add).then_inc(x_updated, 1)

            def step(l, i, parity):
                if not x_ahead(i):
                    run(l, i, parity, 0, copy_x)
                run(l, i, parity, 1, sum_squares, K1)
                if not x_ahead(i):
                    run(l, i, parity, 0, lower_xt)
                run(l, i, parity, 1, clamp_norm, 1)
                run(l, i, parity, 1, copy_v, 0)
                run(l, i, parity, 2, row_max, 2)
                if last_step(i):
                    ffn_stats(l, 0)
                run(l, i, parity, 1, copy_qk, Q1)
                run(l, i, parity, 0, rotary, Q0)
                run(l, i, parity, 2, copy_pT, 0)
                run(l, i, parity, 2, inverse_sum, 2)
                if last_step(i):
                    ffn_normalise(l, 0)
                    ffn_stats(l, 1)
                run(l, i, parity, 1, row_max, 1)
                run(l, i, parity, 0, rotary, K0)
                run(l, i, parity, 0, sum_squares, Q1)
                run(l, i, parity, 0, sum_squares, K0)
                run(l, i, parity, 1, inverse_sum, 1)
                run(l, i, parity, 0, sum_squares, Q0)
                run(l, i, parity, 1, row_max, 0)
                run(l, i, parity, 0, clamp_norm, 0)
                if last_step(i):
                    ffn_affine(l, 0)
                    ffn_lower(l, 0)
                run(l, i, parity, 2, copy_o, 1)
                run(l, i, parity, 0, rotary, Q1)
                run(l, i, parity, 1, inverse_sum, 0)
                run(l, i, parity, 1, row_max, 3)
                if last_step(i):
                    ffn_normalise(l, 1)
                run(l, i, parity, 2, add_residual)
                run(l, i, parity, 0, rotary, K1)
                run(l, i, parity, 1, inverse_sum, 3)

            def ffn_stats(l, q):
                dve.wait_ge(f_shift_ps, l * NQ + q + 1)
                stats(lambda b: ps[:, q % 2, b * P:(b + 1) * P], q)
                aggregate(q, 8 * NQ + 4 * (l * NQ + q + 1), f_var)

            def ffn_normalise(l, q):
                dve.wait_ge(f_rstd, l * NQ + q + 1)
                if q >= 1:
                    dve.wait_ge(f_xhT_ps, l * NQ + q)
                apply(lambda b: xh[:, b, :], lambda b: ps[:, q % 2, b * P:(b + 1) * P], q).then_inc(f_xh, 1)

            def ffn_affine(l, q):
                if q == 0:
                    dve.wait_ge(ld_ffn, 32 * l + 32)
                dve.wait_ge(f_xhT_ps, l * NQ + q + 1)
                V.tensor_scalar(xhT[:, q % 2, :], ps[:, q % 2, :], vec[:, 0:1], vec[:, 1:2], ALU.mult, ALU.add).then_inc(f_xhT, 1)

            def ffn_lower(l, q):
                dve.wait_ge(f_hi, l * NQ + q + 1)
                V.tensor_tensor(xhT_lo[:, q % 2, :], xhT[:, q % 2, :], xhT_hi[:, q % 2, :], ALU.subtract).then_inc(f_lo, 1)

            def ffn_gated(l, q, c):
                j = q * FCH + c
                dve.wait_ge(f_gate, (l * NQ + q) * FCH + c + 1)
                V.scalar_tensor_tensor(out=hT[0:FC, q % 2, c, :], in0=ps[0:FC, 2 + j % 2, :], scalar=vec[0:FC, 2 + c:3 + c],
                                       in1=gate[:, j % 2, :], op0=ALU.add, op1=ALU.mult).then_inc(f_h, 1)

            def ffn_residual(l, q):
                dve.wait_ge(f_y_ps, l * NQ + q + 1)
                w = xr[:, q * QUAD:(q + 1) * QUAD, :]
                V.tensor_tensor(w, w, ps[:, 5, :].rearrange("p (b d) -> p b d", b=QUAD), ALU.add).then_inc(x_final, 1)

            cross_stats_x(0)
            cross_stats_x(1)
            cross_normalise_x(0)
            dve.wait_ge(ld_const, 80)
            V.tensor_copy(band16[:], consts[:, 0:P].unsqueeze(1).broadcast_to([P, 4, P])).then_inc(const_ready, 1)
            dve.wait_ge(const_ready, 8)
            cross_normalise_x(1)
            for q in range(NQ):
                cross_max(q)
                if q >= 1:
                    cross_normalise_out(q - 1)
                cross_normalise_p(q)
                if q + 2 < NQ:
                    cross_stats_x(q + 2)
                    cross_normalise_x(q + 2)
                cross_add(q)
            cross_normalise_out(NQ - 1)

            def layer(l, last):
                n = l + 1
                steps(dve, l, step)
                for q in range(NQ + 1):
                    if 1 <= q < NQ - 1:
                        ffn_normalise(l, q + 1)
                    if q < NQ:
                        ffn_gated(l, q, 0)
                    if q == 3 and not last:
                        rotary(n, 0, 0, K0)
                        sum_squares(n, 0, 0, K0)
                    if q == NQ and not last:
                        sum_squares(n, 0, 0, Q0)
                        clamp_norm(n, 0, 0, 0)
                        rotary(n, 0, 0, Q1)
                    if q >= 1:
                        ffn_residual(l, q - 1)
                        if last:
                            add_input(q - 1)
                    if q == 1 and not last:
                        dve.wait_ge(x_final, n * NQ + 1)
                        copy_x(n, 0, 0)
                        copy_x(n, 1, 1)
                    if q == 2 and not last:
                        lower_xt(n, 0, 0)
                    if q + 1 < NQ:
                        ffn_affine(l, q + 1)
                        ffn_lower(l, q + 1)
                    if q == 3 and not last:
                        rotary(n, 0, 0, Q0)
                    if q < NQ:
                        ffn_gated(l, q, 1)
                        if q + 2 < NQ:
                            ffn_stats(l, q + 2)
                        if q == 2 and not last:
                            rope_tables(n)
                        if q == 3 and not last:
                            lower_xt(n, 1, 1)
                        ffn_gated(l, q, 2)
                if not last:
                    rotary(n, 0, 0, K1)
                    sum_squares(n, 0, 0, Q1)

            def add_input(q):
                s = slice(q * QUAD, (q + 1) * QUAD)
                dve.wait_ge(x_final, L * NQ + q + 1)
                V.tensor_tensor(x1[:, s, :], x1[:, s, :], xr[:, s, :], ALU.add).then_inc(final_sum, 1)

            rope_tables(0)
            copy_x(0, 0, 0)
            copy_x(0, 1, 1)
            lower_xt(0, 0, 0)
            lower_xt(0, 1, 1)
            step(0, 0, 0)
            all_layers(dve, layer)


def kernel(**inputs):
    import concourse.bacc as bacc
    from concourse.bass_utils import run_bass_kernel_spmd

    a = {k: np.ascontiguousarray(np.asarray(w)) for k, w in inputs.items()}
    w1 = np.zeros((L, P, 2, FCH * FC), np.float32)
    w1[:, :, :, :FI] = a["L0_ffn_W1"].reshape(L, P, 2, FI)
    b1 = np.zeros((L, 2, FCH * FC), np.float32)
    b1[:, :, :FI] = a["L0_ffn_b1"].reshape(L, 2, FI)
    w2 = np.zeros((L, FCH * FC, P), np.float32)
    w2[:, :FI] = a["L0_ffn_W2"]
    w2_rows = np.zeros((L, FC + 1, FCH, P), np.float32)
    w2_rows[:, :FC] = w2.reshape(L, FCH, FC, P).transpose(0, 2, 1, 3)
    w2_rows[:, FC, 0] = a["L0_ffn_b2"]
    vec = np.zeros((L, P, 2 + 2 * FCH), np.float32)
    vec[:, :, 0] = a["L0_ffn_ln_g"]
    vec[:, :, 1] = a["L0_ffn_ln_b"]
    vec[:, :FC, 2:] = b1.reshape(L, 2 * FCH, FC).transpose(0, 2, 1)
    rope, const = constants()
    arrays = {
        "x_in": a["x"],
        "ctx_in": a["ctx_1024"],
        "xw_in": np.stack([a["L0_xattn_Wq"], a["L0_xattn_Wk"], a["L0_xattn_Wv"]], 1),
        "xv_in": np.stack([a["L0_xattn_bq"], a["L0_xattn_bk"]], 1),
        "bv_in": a["L0_xattn_bv"].reshape(1, P),
        "wqkv_in": a["L0_ffn_Wqkv"],
        "qk_scale_in": np.stack([a["L0_ffn_q_scale"], a["L0_ffn_k_scale"]], 1),
        "wo_in": a["L0_ffn_Wo"].reshape(L, 8, P, P).transpose(0, 2, 1, 3),
        "w1_in": w1.reshape(L, P, 2 * FCH, FC),
        "w2_in": w2_rows,
        "vec_in": vec,
        "rope_in": rope,
        "const_in": const,
    }
    arrays = {k: np.ascontiguousarray(w) for k, w in arrays.items()}
    nc = bacc.Bacc("TRN2", target_bir_lowering=False, num_devices=1)
    args = [nc.dram_tensor(k, w.shape, F32, kind="ExternalInput").ap() for k, w in arrays.items()]
    out = nc.dram_tensor("out", (B, P, P), F32, kind="ExternalOutput").ap()
    build(nc, *args, out)
    r = run_bass_kernel_spmd(nc, [arrays], core_ids=[0])
    return r.results[0]["out"]
```
